# Optimizing a Trainium2 kernel written in Bass

```python
import numpy as np
import jax
import jax.numpy as jnp

def _softmax(x, axis=-1):
    return jax.nn.softmax(x, axis=axis)

def _gelu(x):
    return jax.nn.gelu(x, approximate=True)

def _silu(x):
    return jax.nn.silu(x)

def _sigmoid(x):
    return jax.nn.sigmoid(x)

def _layernorm(x, axis=-1, eps=1e-05):
    m = jnp.mean(x, axis=axis, keepdims=True)
    v = jnp.var(x, axis=axis, keepdims=True)
    return (x - m) / jnp.sqrt(v + eps)

def _scatter_add(tgt, idx, src, axis=0):
    return tgt.at[idx].add(src)

def _segment_sum(src, seg, n):
    return jax.ops.segment_sum(src, seg, n)
kernel_name = 'mk_cond_resid_d4_seqx_r2_4bebe5'

def setup_inputs(seed: int=0):
    np.random.seed(seed)
    _w = jnp.asarray

    def _rec_inputs():
        import jax
        import jax.numpy as jnp
        _rk = jax.random.key(seed)
        x = -0.000125 + 0.9999 * jax.random.normal(jax.random.fold_in(_rk, 1), (32, 128, 2048), jnp.float32)
        _lenS = 128 - jax.random.randint(jax.random.fold_in(_rk, 7), (32,), 0, max(1, 128 // 4) + 1, jnp.int32)
        _lenS2 = 128 - jax.random.randint(jax.random.fold_in(_rk, 8), (32,), 0, max(1, 128 // 4) + 1, jnp.int32)
        cond_128 = 0.0061147 + 1.02565 * jax.random.normal(jax.random.fold_in(_rk, 11), (32, 128), jnp.float32)
        fside_S_0 = -0.022604 + 0.987366 * jax.random.normal(jax.random.fold_in(_rk, 12), (128,), jnp.float32)
        return (x, cond_128, fside_S_0)
    x, cond_128, fside_S_0 = _rec_inputs()

    def _L0_cond_setup():
        import jax, jax.numpy as jnp
        import numpy as np
        K = 8
        T = 1.0
        D_EMBD = 128
        IN_C = 128
        OUT_C = 128
        BS = 32
        H = 2048
        HID = 128
        key = jax.random.key(seed)
        ks = jax.random.split(key, 10)
        s = lambda fan_in: 1.0 / np.sqrt(fan_in)
        return {'x': jax.random.normal(ks[0], (BS, IN_C, H), dtype=jnp.float32), 'embedding': jax.random.normal(ks[1], (BS, D_EMBD), dtype=jnp.float32), 'W0': jax.random.normal(ks[2], (D_EMBD, HID), dtype=jnp.float32) * s(D_EMBD), 'b0': jnp.zeros((HID,), dtype=jnp.float32), 'W1': jax.random.normal(ks[3], (HID, HID), dtype=jnp.float32) * s(HID), 'b1': jnp.zeros((HID,), dtype=jnp.float32), 'W2': jax.random.normal(ks[4], (HID, K), dtype=jnp.float32) * s(HID), 'b2': jnp.zeros((K,), dtype=jnp.float32), 'weight': jax.random.normal(ks[5], (K, OUT_C, IN_C, 1), dtype=jnp.float32) * s(IN_C), 'bias_k': jax.random.normal(ks[6], (K, OUT_C), dtype=jnp.float32) * 0.1}
    _L0_cond_all = _L0_cond_setup()
    _L0_cond_in = {k: v for k, v in _L0_cond_all.items() if k in ('W0', 'b0', 'W1', 'b1', 'W2', 'b2', 'weight', 'bias_k')}
    del _L0_cond_all

    def _L1_cond_setup():
        import jax, jax.numpy as jnp
        import numpy as np
        from jax import lax
        N, C_IN, L = (32, 128, 2048)
        C_OUT, K, GROUPS = (128, 9, 4)
        C_DIM, PAD, STRIDE = (128, 4, 1)
        key = jax.random.key(seed)
        k1, k2, k3, k4, k5 = jax.random.split(key, 5)
        x = jax.random.normal(k1, (N, C_IN, L), dtype=jnp.float32)
        c = jax.random.normal(k2, (N, C_DIM), dtype=jnp.float32)
        weight = jax.random.normal(k3, (C_OUT, C_IN // GROUPS, K), dtype=jnp.float32)
        c_weight = jax.random.normal(k4, (C_OUT, C_DIM), dtype=jnp.float32)
        bias = jax.random.normal(k5, (C_OUT,), dtype=jnp.float32)
        return {'x': x, 'c': c, 'weight': weight, 'c_weight': c_weight, 'bias': bias}
    _L1_cond_all = _L1_cond_setup()
    _L1_cond_in = {k: v for k, v in _L1_cond_all.items() if k in ('weight', 'c_weight')}
    del _L1_cond_all

    def _L2_cond_setup():
        import jax, jax.numpy as jnp
        import numpy as np
        K = 8
        T = 1.0
        D_EMBD = 128
        IN_C = 128
        OUT_C = 128
        BS = 32
        H = 2048
        HID = 128
        key = jax.random.key(seed)
        ks = jax.random.split(key, 10)
        s = lambda fan_in: 1.0 / np.sqrt(fan_in)
        return {'x': jax.random.normal(ks[0], (BS, IN_C, H), dtype=jnp.float32), 'embedding': jax.random.normal(ks[1], (BS, D_EMBD), dtype=jnp.float32), 'W0': jax.random.normal(ks[2], (D_EMBD, HID), dtype=jnp.float32) * s(D_EMBD), 'b0': jnp.zeros((HID,), dtype=jnp.float32), 'W1': jax.random.normal(ks[3], (HID, HID), dtype=jnp.float32) * s(HID), 'b1': jnp.zeros((HID,), dtype=jnp.float32), 'W2': jax.random.normal(ks[4], (HID, K), dtype=jnp.float32) * s(HID), 'b2': jnp.zeros((K,), dtype=jnp.float32), 'weight': jax.random.normal(ks[5], (K, OUT_C, IN_C, 1), dtype=jnp.float32) * s(IN_C), 'bias_k': jax.random.normal(ks[6], (K, OUT_C), dtype=jnp.float32) * 0.1}
    _L2_cond_all = _L2_cond_setup()
    _L2_cond_in = {k: v for k, v in _L2_cond_all.items() if k in ('W0', 'b0', 'W1', 'b1', 'W2', 'b2', 'weight', 'bias_k')}
    del _L2_cond_all

    def _L3_cond_setup():
        import jax, jax.numpy as jnp
        import numpy as np
        K = 8
        T = 1.0
        D_EMBD = 128
        IN_C = 128
        OUT_C = 128
        BS = 32
        H = 2048
        HID = 128
        key = jax.random.key(seed)
        ks = jax.random.split(key, 10)
        s = lambda fan_in: 1.0 / np.sqrt(fan_in)
        return {'x': jax.random.normal(ks[0], (BS, IN_C, H), dtype=jnp.float32), 'embedding': jax.random.normal(ks[1], (BS, D_EMBD), dtype=jnp.float32), 'W0': jax.random.normal(ks[2], (D_EMBD, HID), dtype=jnp.float32) * s(D_EMBD), 'b0': jnp.zeros((HID,), dtype=jnp.float32), 'W1': jax.random.normal(ks[3], (HID, HID), dtype=jnp.float32) * s(HID), 'b1': jnp.zeros((HID,), dtype=jnp.float32), 'W2': jax.random.normal(ks[4], (HID, K), dtype=jnp.float32) * s(HID), 'b2': jnp.zeros((K,), dtype=jnp.float32), 'weight': jax.random.normal(ks[5], (K, OUT_C, IN_C, 1), dtype=jnp.float32) * s(IN_C), 'bias_k': jax.random.normal(ks[6], (K, OUT_C), dtype=jnp.float32) * 0.1}
    _L3_cond_all = _L3_cond_setup()
    _L3_cond_in = {k: v for k, v in _L3_cond_all.items() if k in ('W0', 'b0', 'W1', 'b1', 'W2', 'b2', 'weight', 'bias_k')}
    del _L3_cond_all
    return {'x': x, 'cond_128': cond_128, 'fside_S_0': fside_S_0, 'L0_cond_W0': _L0_cond_in['W0'], 'L0_cond_b0': _L0_cond_in['b0'], 'L0_cond_W1': _L0_cond_in['W1'], 'L0_cond_b1': _L0_cond_in['b1'], 'L0_cond_W2': _L0_cond_in['W2'], 'L0_cond_b2': _L0_cond_in['b2'], 'L0_cond_weight': _L0_cond_in['weight'], 'L0_cond_bias_k': _L0_cond_in['bias_k'], 'L1_cond_weight': _L1_cond_in['weight'], 'L1_cond_c_weight': _L1_cond_in['c_weight'], 'L2_cond_W0': _L2_cond_in['W0'], 'L2_cond_b0': _L2_cond_in['b0'], 'L2_cond_W1': _L2_cond_in['W1'], 'L2_cond_b1': _L2_cond_in['b1'], 'L2_cond_W2': _L2_cond_in['W2'], 'L2_cond_b2': _L2_cond_in['b2'], 'L2_cond_weight': _L2_cond_in['weight'], 'L2_cond_bias_k': _L2_cond_in['bias_k'], 'L3_cond_W0': _L3_cond_in['W0'], 'L3_cond_b0': _L3_cond_in['b0'], 'L3_cond_W1': _L3_cond_in['W1'], 'L3_cond_b1': _L3_cond_in['b1'], 'L3_cond_W2': _L3_cond_in['W2'], 'L3_cond_b2': _L3_cond_in['b2'], 'L3_cond_weight': _L3_cond_in['weight'], 'L3_cond_bias_k': _L3_cond_in['bias_k']}

def reference(x, cond_128, fside_S_0, L0_cond_W0, L0_cond_b0, L0_cond_W1, L0_cond_b1, L0_cond_W2, L0_cond_b2, L0_cond_weight, L0_cond_bias_k, L1_cond_weight, L1_cond_c_weight, L2_cond_W0, L2_cond_b0, L2_cond_W1, L2_cond_b1, L2_cond_W2, L2_cond_b2, L2_cond_weight, L2_cond_bias_k, L3_cond_W0, L3_cond_b0, L3_cond_W1, L3_cond_b1, L3_cond_W2, L3_cond_b2, L3_cond_weight, L3_cond_bias_k):
    import jax
    import jax.numpy as jnp

    def _L0_cond_ref(x, embedding, W0, b0, W1, b1, W2, b2, weight, bias_k):
        import jax, jax.numpy as jnp
        import numpy as np
        K = 8
        T = 1.0
        D_EMBD = 128
        IN_C = 128
        OUT_C = 128
        BS = 32
        H = 2048
        HID = 128
        h = jax.nn.gelu(embedding @ W0 + b0, approximate=False)
        h = jax.nn.gelu(h @ W1 + b1, approximate=False)
        att = jax.nn.softmax((h @ W2 + b2) / T, axis=-1)
        agg_w = jnp.einsum('bk,koi->boi', att, weight[..., 0])
        agg_b = att @ bias_k
        out = jnp.einsum('boi,bih->boh', agg_w, x) + agg_b[:, :, None]
        return out

    def _L1_cond_ref(x, c, weight, c_weight, bias):
        import jax, jax.numpy as jnp
        import numpy as np
        from jax import lax
        N, C_IN, L = (32, 128, 2048)
        C_OUT, K, GROUPS = (128, 9, 4)
        C_DIM, PAD, STRIDE = (128, 4, 1)
        out = lax.conv_general_dilated(x, weight, window_strides=(STRIDE,), padding=[(PAD, PAD)], dimension_numbers=('NCH', 'OIH', 'NCH'), feature_group_count=GROUPS)
        ctx = jnp.einsum('nd,od->no', c, c_weight)
        out = out + ctx[:, :, None] + bias[None, :, None]
        return out

    def _L2_cond_ref(x, embedding, W0, b0, W1, b1, W2, b2, weight, bias_k):
        import jax, jax.numpy as jnp
        import numpy as np
        K = 8
        T = 1.0
        D_EMBD = 128
        IN_C = 128
        OUT_C = 128
        BS = 32
        H = 2048
        HID = 128
        h = jax.nn.gelu(embedding @ W0 + b0, approximate=False)
        h = jax.nn.gelu(h @ W1 + b1, approximate=False)
        att = jax.nn.softmax((h @ W2 + b2) / T, axis=-1)
        agg_w = jnp.einsum('bk,koi->boi', att, weight[..., 0])
        agg_b = att @ bias_k
        out = jnp.einsum('boi,bih->boh', agg_w, x) + agg_b[:, :, None]
        return out

    def _L3_cond_ref(x, embedding, W0, b0, W1, b1, W2, b2, weight, bias_k):
        import jax, jax.numpy as jnp
        import numpy as np
        K = 8
        T = 1.0
        D_EMBD = 128
        IN_C = 128
        OUT_C = 128
        BS = 32
        H = 2048
        HID = 128
        h = jax.nn.gelu(embedding @ W0 + b0, approximate=False)
        h = jax.nn.gelu(h @ W1 + b1, approximate=False)
        att = jax.nn.softmax((h @ W2 + b2) / T, axis=-1)
        agg_w = jnp.einsum('bk,koi->boi', att, weight[..., 0])
        agg_b = att @ bias_k
        out = jnp.einsum('boi,bih->boh', agg_w, x) + agg_b[:, :, None]
        return out
    x = x + _L0_cond_ref(x, cond_128, L0_cond_W0, L0_cond_b0, L0_cond_W1, L0_cond_b1, L0_cond_W2, L0_cond_b2, L0_cond_weight, L0_cond_bias_k)
    x = x + _L1_cond_ref(x, cond_128, L1_cond_weight, L1_cond_c_weight, fside_S_0)
    x = x + _L2_cond_ref(x, cond_128, L2_cond_W0, L2_cond_b0, L2_cond_W1, L2_cond_b1, L2_cond_W2, L2_cond_b2, L2_cond_weight, L2_cond_bias_k)
    x = x + _L3_cond_ref(x, cond_128, L3_cond_W0, L3_cond_b0, L3_cond_W1, L3_cond_b1, L3_cond_W2, L3_cond_b2, L3_cond_weight, L3_cond_bias_k)
    return x

_drawn_inputs = setup_inputs


def setup_inputs(seed=0):
    import zlib

    import numpy as np

    out = dict(_drawn_inputs(seed))
    spreads = {'L0_cond_b0': (0.0, 0.728),
     'L0_cond_b1': (0.0, 0.447),
     'L0_cond_b2': (0.0, 0.416),
     'L2_cond_b0': (0.0, 0.747),
     'L2_cond_b1': (0.0, 0.385),
     'L2_cond_b2': (0.0, 0.44),
     'L3_cond_b0': (0.0, 0.613),
     'L3_cond_b1': (0.0, 0.398),
     'L3_cond_b2': (0.0, 0.311)}
    factors = {'L2_cond_bias_k': 36.771, 'L3_cond_bias_k': 40.863}
    for name, (base, spread) in spreads.items():
        noise = np.random.default_rng([zlib.crc32(name.encode()), seed]).standard_normal(out[name].shape)
        drawn = base * np.exp(spread * noise) if base else spread * noise
        out[name] = jnp.asarray(drawn.astype(out[name].dtype))
    for name, factor in factors.items():
        out[name] = (out[name] * factor).astype(out[name].dtype)
    return out
```

```python
from contextlib import ExitStack

import concourse.bass as bass
from concourse import mybir

F32 = mybir.dt.float32
F32R = mybir.dt.float32r
ALU = mybir.AluOpType
ACT = mybir.ActivationFunctionType
AX_X = mybir.AxisListType.X

P = 128
B = 32
L = 2048
K = 8
PH = 4
G = 4
CG = P // G
T = L // PH
TAPS = 9
SHIFTS = 3
NL = 3
DMA = 16
REMAPS = G * PH

FIRST, LAST = -2, B + 1
C_ATT0, C_ATT23, C_C0, C_D, C_C2, C_C3 = 0, K, 3 * K, 3 * K + G, 3 * K + 2 * G, 3 * K + 2 * G + 1
COLS = 3 * K + 2 * G + 2
ROWS = LAST - FIRST + 1
LOOP_FROM, LOOP_TO = 4, B - 3

ERF_P = [-2.72614225801306e-10, 2.77068142495902e-08, -2.10102402082508e-06, -5.69250639462346e-05,
         -7.34990630326855e-04, -2.95459980854025e-03, -1.60960333262415e-02]
ERF_Q = [-1.45660718464996e-05, -2.13374055278905e-04, -1.68282697438203e-03, -7.37332916720468e-03,
         -1.42647390514189e-02]


class Slot:

    def __init__(self, i, r):
        self.i, self.r = i, r
        self.known = isinstance(i, int)

    def count(self, per, ahead, extra):
        return self.i * (2 * per) + (per * (self.r + ahead) + extra)

    def pairs(self, per, ahead):
        return self.i * per + per * ((self.r + ahead) // 2)

    def parity(self, ahead):
        return (self.r + ahead) % 2

    def batch(self, ahead):
        return self.i * 2 + (self.r + ahead)

    def has(self, ahead):
        return not self.known or 0 <= 2 * self.i + self.r + ahead < B


def wait(eng, semaphore, value):
    if not isinstance(value, int) or value > 0:
        eng.wait_ge(semaphore, value)


def run_slots(eng, body):
    for b in range(FIRST, LOOP_FROM):
        body(Slot(b // 2, b % 2))
    with eng.Fori(LOOP_FROM // 2, (LOOP_TO + 1) // 2) as i:
        body(Slot(i, 0))
        body(Slot(i, 1))
    for b in range(LOOP_TO + 1, LAST + 1):
        body(Slot(b // 2, b % 2))


def cond_resid_kernel(nc, x, cond_t, w0, w1, w2, b0, b1, b2, mix, bias0, bias2, bias3, conv, c_weight,
                      fside, eye, out):
    with ExitStack() as ctx:
        def sb(name, shape, dt=F32):
            return ctx.enter_context(nc.sbuf_tensor(name, shape, dt))

        def sem(name):
            return ctx.enter_context(nc.semaphore(name))

        cond_sb = sb("cond_sb", [P, B])
        w0_sb = sb("w0_sb", [P, NL, P])
        w1_sb = sb("w1_sb", [P, NL, P])
        w2_sb = sb("w2_sb", [P, NL, K])
        b0_sb = sb("b0_sb", [P, NL])
        b1_sb = sb("b1_sb", [P, NL])
        b2_sb = sb("b2_sb", [1, NL * K])
        mix_sb = sb("mix_sb", [P, NL, K, P])
        bias0_sb = sb("bias0_sb", [K, G, P])
        bias2_sb = sb("bias2_sb", [K, P])
        bias3_sb = sb("bias3_sb", [K, P])
        cw_sb = sb("cw_sb", [P, G, P])
        fside_sb = sb("fside_sb", [1, G, P])
        eye_sb = sb("eye_sb", [P, P])
        ones_sb = sb("ones_sb", [B, P])
        conv_f = sb("conv_f", [P, G, SHIFTS, P])
        conv_hi = sb("conv_hi", [P, G, SHIFTS, P], F32R)
        conv_lo = sb("conv_lo", [P, G, SHIFTS, P], F32R)
        pre = sb("pre", [P, NL, B])
        arg = sb("arg", [P, NL, B])
        sq = sb("sq", [P, NL, B])
        num = sb("num", [P, NL, B])
        den = sb("den", [P, NL, B])
        hid0 = sb("hid0", [P, NL, B])
        hid1 = sb("hid1", [P, NL, B])
        lmax = sb("lmax", [B, NL])
        lsub = sb("lsub", [B, NL, K])
        lexp = sb("lexp", [B, NL, K])
        lsum = sb("lsum", [B, NL])
        linv = sb("linv", [B, NL])
        att = sb("att", [B, NL, K])
        att_diag = sb("att_diag", [B, NL, B, K])
        att_t = sb("att_t", [K, NL, B])
        table = sb("table", [P, ROWS, COLS])
        cur = [sb(f"cur{j}", [P, COLS]) for j in range(2)]
        a0 = [sb(f"a0_{j}", [P, P]) for j in range(2)]
        a2 = [sb(f"a2_{j}", [P, P]) for j in range(2)]
        a3 = [sb(f"a3_{j}", [P, P]) for j in range(2)]
        m_hi = [sb(f"m_hi{j}", [P, P], F32R) for j in range(2)]
        m_lo = [sb(f"m_lo{j}", [P, P], F32R) for j in range(2)]
        e_col = [sb(f"e_col{j}", [P, 1]) for j in range(2)]
        x_sb = [sb(f"x_sb{j}", [P, PH, T]) for j in range(2)]
        x1_hi = [sb(f"x1_hi{j}", [P, G, T + 2], F32R) for j in range(2)]
        x1_lo = [sb(f"x1_lo{j}", [P, G, T + 2], F32R) for j in range(2)]
        x2_poly = [sb(f"x2_poly{j}", [P, G, T]) for j in range(2)]
        x2_chan = [sb(f"x2_chan{j}", [P, PH, T]) for j in range(2)]
        x2_hi = [sb(f"x2_hi{j}", [P, PH, T], F32R) for j in range(2)]
        x2_lo = [sb(f"x2_lo{j}", [P, PH, T], F32R) for j in range(2)]
        y_sb = [sb(f"y_sb{j}", [P, PH, T]) for j in range(2)]

        def bank(name):
            return ctx.enter_context(nc.psum_tensor(name, [P, 512], F32))

        l0_ps = [bank(f"l0_ps{j}") for j in range(2)]
        cv_ps = [bank(f"cv_ps{j}") for j in range(2)]
        y_ps = [bank(f"y_ps{j}") for j in range(2)]
        m_ps = bank("m_ps")
        net_ps = bank("net_ps")

        net_loaded = sem("net_loaded")
        mix_loaded = sem("mix_loaded")
        bias_loaded = sem("bias_loaded")
        conv_loaded = sem("conv_loaded")
        x_loaded = [sem(f"x_loaded{j}") for j in range(2)]
        remapped = [sem(f"remapped{j}") for j in range(2)]
        stored = [sem(f"stored{j}") for j in range(2)]
        ones_set = sem("ones_set")
        setup_step = sem("setup_step")
        setup_pe = sem("setup_pe")
        exp_done = sem("exp_done")
        att_in_table = sem("att_in_table")
        bias_in_table = sem("bias_in_table")
        zero_cols = sem("zero_cols")
        conv_split = sem("conv_split")
        cur_set = sem("cur_set")
        mixed0 = sem("mixed0")
        mixed23 = sem("mixed23")
        l0_done = sem("l0_done")
        x1_hi_done = sem("x1_hi_done")
        x1_lo_done = sem("x1_lo_done")
        conv_done = sem("conv_done")
        x2_done = sem("x2_done")
        x2_hi_done = sem("x2_hi_done")
        x2_lo_done = sem("x2_lo_done")
        m_done = sem("m_done")
        m_hi_done = sem("m_hi_done")
        m_lo_done = sem("m_lo_done")
        y_done = sem("y_done")
        y_out = sem("y_out")

        block = ctx.enter_context(nc.Block())

        @block.sync
        def _(sp):
            for dst, src in ((cond_sb, cond_t), (w0_sb, w0), (b0_sb, b0), (w1_sb, w1), (b1_sb, b1), (w2_sb, w2),
                             (b2_sb, b2)):
                sp.dma_start(dst[:], src).then_inc(net_loaded, DMA)
            sp.dma_start(eye_sb[:], eye).then_inc(mix_loaded, DMA)
            sp.dma_start(mix_sb[:], mix).then_inc(mix_loaded, DMA)
            for dst, src in ((bias0_sb, bias0), (bias2_sb, bias2), (bias3_sb, bias3), (cw_sb, c_weight),
                             (fside_sb, fside)):
                sp.dma_start(dst[:], src).then_inc(bias_loaded, DMA)

            def slot(s):
                if s.has(2):
                    wait(sp, l0_done, s.count(G, 0, G))
                    sp.dma_start(x_sb[s.parity(2)][:], x[bass.ds(s.batch(2), 1)].rearrange(
                        "b c q t -> c (b q) t")).then_inc(x_loaded[s.parity(2)], DMA)
                if s.known and 2 * s.i + s.r == FIRST:
                    sp.dma_start(conv_f[:], conv).then_inc(conv_loaded, DMA)
                if s.has(-3):
                    wait(sp, y_out, s.count(PH, -3, PH))
                    sp.dma_start(out[bass.ds(s.batch(-3), 1)].rearrange("b c q t -> c (b q) t"),
                                 y_sb[s.parity(-3)][:]).then_inc(stored[s.parity(-3)], DMA)
                if s.has(0):
                    j = s.parity(0)
                    for g in range(G):
                        wait(sp, x2_done, s.count(G, 0, g + 1))
                        for p in range(PH):
                            sp.dma_start(x2_chan[j][CG * g:CG * (g + 1), p, :],
                                         x2_poly[j][CG * p:CG * (p + 1), g, :]).then_inc(remapped[j], DMA)

            run_slots(sp, slot)
            s = Slot((LAST + 1) // 2, (LAST + 1) % 2)
            sp.wait_ge(y_out, PH * B)
            sp.dma_start(out[B - 1], y_sb[s.parity(-3)][:]).then_inc(stored[s.parity(-3)], DMA)
            for j in range(2):
                sp.wait_ge(stored[j], DMA * (B // 2))

        @block.tensor
        def _(pe):
            pe.wait_ge(net_loaded, 7 * DMA)
            for n in range(NL):
                mm = pe.matmul(net_ps[:, B * n:B * (n + 1)], w0_sb[:, n, :], cond_sb[:], start=True, stop=True)
            mm.then_inc(setup_pe, 1)
            pe.wait_ge(setup_step, HID0)
            for n in range(NL):
                mm = pe.matmul(m_ps[:, B * n:B * (n + 1)], w1_sb[:, n, :], hid0[:, n, :], start=True, stop=True)
            mm.then_inc(setup_pe, 1)
            pe.wait_ge(ones_set, 1)
            pe.matmul(net_ps[0:B, 128:128 + NL * K], ones_sb[0:1, 0:B], b2_sb[:], start=True, stop=False,
                      skip_group_check=True)
            pe.wait_ge(setup_step, HID1)
            for n in range(NL):
                mm = pe.matmul(net_ps[0:B, 128 + K * n:128 + K * (n + 1)], hid1[:, n, :], w2_sb[:, n, :],
                               start=False, stop=True, skip_group_check=True)
            mm.then_inc(setup_pe, 1)
            pe.wait_ge(setup_step, DIAG)
            for n, ps in enumerate((l0_ps[0], l0_ps[1], cv_ps[0])):
                mm = pe.matmul(ps[:, 0:B * K], ones_sb[:], att_diag[:, n].rearrange("a b k -> a (b k)"),
                               start=True, stop=True)
            mm.then_inc(setup_pe, 1)
            pe.wait_ge(mix_loaded, 2 * DMA)
            for n in range(NL):
                mm = pe.transpose(m_ps[0:K, 128 + B * n:128 + B * (n + 1)], att[:, n, :], eye_sb[0:B, 0:B])
            mm.then_inc(setup_pe, 1)
            pe.wait_ge(bias_loaded, 5 * DMA)
            for g in range(G):
                pe.matmul(y_ps[1][:, B * g:B * (g + 1)], cw_sb[:, g, :], cond_sb[:], start=True, stop=False)
                mm = pe.matmul(y_ps[1][:, B * g:B * (g + 1)], fside_sb[:, g, :], ones_sb[0:1, 0:B],
                               start=False, stop=True)
            pe.wait_ge(setup_step, ATT_T)
            for g in range(G):
                pe.matmul(y_ps[0][:, B * g:B * (g + 1)], bias0_sb[:, g, :], att_t[:, 0, :], start=True, stop=True)
            pe.matmul(y_ps[0][:, B * G:B * (G + 1)], bias2_sb[:], att_t[:, 1, :], start=True, stop=True)
            mm = pe.matmul(y_ps[0][:, B * (G + 1):B * (G + 2)], bias3_sb[:], att_t[:, 2, :], start=True, stop=True)
            mm.then_inc(setup_pe, 1)

            def layer0(s, g):
                if g == 0:
                    pe.wait_ge(x_loaded[s.parity(1)], s.pairs(DMA, 3))
                    pe.wait_ge(mixed0, s.count(K, 1, K))
                wait(pe, x1_lo_done, s.count(G, 1, g - 1))
                for q in range(PH):
                    mm = pe.matmul(l0_ps[g % 2][CG * q:CG * (q + 1), 0:T], a0[s.parity(1)][:, CG * g:CG * (g + 1)],
                                   x_sb[s.parity(1)][:, q, :], start=True, stop=True)
                mm.then_inc(l0_done, 1)

            def convolve(s, g):
                j = s.parity(0)
                pe.wait_ge(x1_lo_done, s.count(G, 0, g + 1))
                if s.known and 2 * s.i + s.r == 0 and g == 0:
                    pe.wait_ge(conv_split, 2)
                    pe.wait_ge(zero_cols, 4)
                wait(pe, x2_done, s.count(G, 0, g - 1))
                n = 0
                for sh in range(SHIFTS):
                    for w, a in ((conv_hi, x1_hi), (conv_lo, x1_hi), (conv_hi, x1_lo)):
                        mm = pe.matmul(cv_ps[g % 2][:, 0:T], w[:, g, sh, :], a[j][:, g, sh:sh + T],
                                       start=(n == 0), stop=(n == 3 * SHIFTS - 1))
                        n += 1
                mm.then_inc(conv_done, 1)

            def product(s):
                j = s.parity(-2)
                pe.wait_ge(cur_set, s.count(1, 0, 3))
                pe.wait_ge(mixed23, s.count(2 * K, -2, 2 * K))
                wait(pe, m_lo_done, s.count(1, -2, 0))
                pe.matmul(m_ps[:, 0:P], a2[j][:], a3[j][:], start=True, stop=True)
                pe.matmul(m_ps[:, P:P + 1], a3[j][:], cur[s.parity(0)][:, C_C2:C_C2 + 1],
                          start=True, stop=True).then_inc(m_done, 1)

            def output(s, p):
                j = s.parity(-2)
                if p == 0:
                    pe.wait_ge(m_lo_done, s.count(1, -2, 1))
                pe.wait_ge(x2_lo_done, s.count(PH, -2, p + 1))
                wait(pe, y_out, s.count(PH, -2, p - 1))
                for n, (w, a) in enumerate(((m_hi, x2_hi), (m_lo, x2_hi), (m_hi, x2_lo))):
                    mm = pe.matmul(y_ps[p % 2][:, 0:T], w[j][:], a[j][:, p, :], start=(n == 0), stop=(n == 2))
                mm.then_inc(y_done, 1)

            def slot(s):
                if s.has(-2):
                    product(s)
                for g in range(G):
                    if s.has(1):
                        layer0(s, g)
                    if s.has(0):
                        convolve(s, g)
                    if s.has(-2):
                        output(s, g)

            run_slots(pe, slot)

        @block.scalar
        def _(act):
            act.wait_ge(setup_step, LSUB)
            nc.scalar.activation(lexp[:], lsub[:], ACT.Exp).then_inc(exp_done, 1)

            def split(s, p):
                j = s.parity(-1)
                if p == 0:
                    act.wait_ge(remapped[j], s.pairs(DMA * REMAPS, 1))
                wait(act, y_done, s.count(PH, -3, p + 1))
                nc.scalar.activation(x2_hi[j][:, p, :], x2_chan[j][:, p, :], ACT.Identity).then_inc(x2_hi_done, 1)

            def slot(s):
                c = cur[s.parity(0)]
                act.wait_ge(cur_set, s.count(1, 0, 3))
                if s.has(-2):
                    j = s.parity(-2)
                    act.wait_ge(m_done, s.count(1, -2, 1))
                    wait(act, y_done, s.count(PH, -4, PH))
                    nc.scalar.activation(m_hi[j][:], m_ps[:, 0:P], ACT.Identity).then_inc(m_hi_done, 1)
                for g in range(G):
                    if s.has(1):
                        act.wait_ge(l0_done, s.count(G, 1, g + 1))
                        wait(act, conv_done, s.count(G, -1, g + 1))
                        nc.scalar.activation(x1_hi[s.parity(1)][:, g, 1:T + 1], l0_ps[g % 2][:, 0:T], ACT.Identity,
                                             bias=c[:, C_C0 + g:C_C0 + g + 1]).then_inc(x1_hi_done, 1)
                    if s.has(-1) and g > 0:
                        split(s, g - 1)
                    if s.has(0):
                        j = s.parity(0)
                        act.wait_ge(conv_done, s.count(G, 0, g + 1))
                        if g == 0:
                            wait(act, remapped[j], s.pairs(DMA * REMAPS, 0))
                            wait(act, x2_lo_done, s.count(PH, -2, PH))
                        nc.scalar.activation(x2_poly[j][:, g, :], cv_ps[g % 2][:, 0:T], ACT.Identity,
                                             bias=c[:, C_D + g:C_D + g + 1]).then_inc(x2_done, 1)
                    if s.has(-2):
                        j = s.parity(-2)
                        act.wait_ge(y_done, s.count(PH, -2, g + 1))
                        if g == 0:
                            act.wait_ge(m_lo_done, s.count(1, -2, 1))
                            wait(act, stored[j], s.pairs(DMA, -2))
                        nc.scalar.activation(y_sb[j][:, g, :], y_ps[g % 2][:, 0:T], ACT.Identity,
                                             bias=e_col[j][:, 0:1]).then_inc(y_out, 1)
                if s.has(-1):
                    split(s, PH - 1)

            run_slots(act, slot)

        @block.gpsimd
        def _(pool):
            nc.gpsimd.memset(ones_sb[:], 1.0).then_inc(ones_set, 1)
            for j in range(2):
                for buf in (x1_hi[j], x1_lo[j]):
                    nc.gpsimd.memset(buf[:, :, 0:T + 2:T + 1].bitcast(F32), 0.0).then_inc(zero_cols, 1)

            def set_cur(s, ahead):
                if s.known and 2 * s.i + s.r + ahead == FIRST + 1:
                    pool.wait_ge(bias_in_table, 4)
                if s.has(ahead - 1):
                    wait(pool, x1_lo_done, s.count(G, ahead - 1, G))
                if s.has(ahead - 2):
                    wait(pool, x2_done, s.count(G, ahead - 2, G))
                if s.has(ahead):
                    wait(pool, mixed0, s.count(K, ahead, K))
                if s.has(ahead - 3):
                    wait(pool, mixed23, s.count(2 * K, ahead - 3, 2 * K))
                if s.has(ahead - 4):
                    wait(pool, m_lo_done, s.count(1, ahead - 4, 1))
                row = s.batch(ahead - FIRST)
                nc.gpsimd.tensor_copy(cur[s.parity(ahead)][:].rearrange("p (a c) -> p a c", a=1),
                                      table[:, bass.ds(row, 1), :]).then_inc(cur_set, 1)

            pool.wait_ge(att_in_table, 3)
            nc.gpsimd.tensor_copy(cur[FIRST % 2][:], table[:, 0, :]).then_inc(cur_set, 1)

            def slot(s):
                if not s.known or 2 * s.i + s.r < LAST:
                    set_cur(s, 1)
                if s.has(-1):
                    j = s.parity(-1)
                    for p in range(PH):
                        pool.wait_ge(x2_hi_done, s.count(PH, -1, p + 1))
                        if p == 0:
                            pool.wait_ge(remapped[j], s.pairs(DMA * REMAPS, 1))
                        wait(pool, y_done, s.count(PH, -3, p + 1))
                        nc.gpsimd.tensor_tensor(x2_lo[j][:, p, :], x2_chan[j][:, p, :], x2_hi[j][:, p, :].bitcast(F32),
                                                ALU.subtract).then_inc(x2_lo_done, 1)

            run_slots(pool, slot)

        @block.vector
        def _(dve):
            steps = [0]

            def step(ins):
                steps[0] += 1
                ins.then_inc(setup_step, 1)
                dve.wait_ge(setup_step, steps[0])

            def gelu(ps, bias, to):
                for n in range(NL):
                    ins = nc.vector.tensor_scalar(pre[:, n, :], ps[:, B * n:B * (n + 1)], bias[:, n:n + 1], None, ALU.add)
                    ins.then_inc(setup_step, 1)
                    steps[0] += 1
                dve.wait_ge(setup_step, steps[0])
                step(nc.vector.tensor_scalar(arg[:], pre[:], 0.7071067811865476, 4.0, ALU.mult, ALU.min))
                step(nc.vector.tensor_scalar(arg[:], arg[:], -4.0, None, ALU.max))
                step(nc.vector.tensor_tensor(sq[:], arg[:], arg[:], ALU.mult))
                step(nc.vector.tensor_scalar(num[:], sq[:], ERF_P[0], ERF_P[1], ALU.mult, ALU.add))
                step(nc.vector.tensor_scalar(den[:], sq[:], ERF_Q[0], ERF_Q[1], ALU.mult, ALU.add))
                step(nc.vector.tensor_tensor(num[:], num[:], sq[:], ALU.mult))
                for c in ERF_P[2:-1]:
                    step(nc.vector.scalar_tensor_tensor(out=num[:], in0=num[:], scalar=c, in1=sq[:], op0=ALU.add,
                                                        op1=ALU.mult))
                step(nc.vector.scalar_tensor_tensor(out=num[:], in0=num[:], scalar=ERF_P[-1], in1=arg[:], op0=ALU.add,
                                                    op1=ALU.mult))
                step(nc.vector.tensor_tensor(den[:], den[:], sq[:], ALU.mult))
                for c in ERF_Q[2:-1]:
                    step(nc.vector.scalar_tensor_tensor(out=den[:], in0=den[:], scalar=c, in1=sq[:], op0=ALU.add,
                                                        op1=ALU.mult))
                step(nc.vector.tensor_scalar(den[:], den[:], ERF_Q[-1], None, ALU.add))
                step(nc.vector.reciprocal(den[:], den[:]))
                step(nc.vector.tensor_tensor(num[:], num[:], den[:], ALU.mult))
                step(nc.vector.tensor_scalar(num[:], num[:], 1.0, 0.5, ALU.add, ALU.mult))
                step(nc.vector.tensor_tensor(to[:], num[:], pre[:], ALU.mult))

            step(nc.vector.memset(table[:], 0.0))
            dve.wait_ge(net_loaded, 7 * DMA)
            dve.wait_ge(setup_pe, 1)
            gelu(net_ps, b0_sb, hid0)
            assert steps[0] == HID0
            dve.wait_ge(setup_pe, 2)
            gelu(m_ps, b1_sb, hid1)
            assert steps[0] == HID1
            dve.wait_ge(setup_pe, 3)
            logits = net_ps[0:B, 128:128 + NL * K].rearrange("b (n k) -> b n k", n=NL)
            step(nc.vector.tensor_reduce(lmax[:], logits, AX_X, ALU.max))
            step(nc.vector.tensor_tensor(lsub[:], logits, lmax[:].unsqueeze(2).to_broadcast([B, NL, K]), ALU.subtract))
            assert steps[0] == LSUB
            dve.wait_ge(exp_done, 1)
            step(nc.vector.tensor_reduce(lsum[:], lexp[:], AX_X, ALU.add))
            step(nc.vector.reciprocal(linv[:], lsum[:]))
            step(nc.vector.tensor_tensor(att[:], lexp[:], linv[:].unsqueeze(2).to_broadcast([B, NL, K]), ALU.mult))
            dve.wait_ge(mix_loaded, 2 * DMA)
            for n in range(NL):
                step(nc.vector.tensor_tensor(att_diag[:, n], att[:, n, :].unsqueeze(1).to_broadcast([B, B, K]),
                                             eye_sb[0:B, 0:B].unsqueeze(2).to_broadcast([B, B, K]), ALU.mult))
            assert steps[0] == DIAG
            dve.wait_ge(setup_pe, 4)
            for ps, row, col in ((l0_ps[0], 0, C_ATT0), (l0_ps[1], 3, C_ATT23), (cv_ps[0], 3, C_ATT23 + K)):
                nc.vector.tensor_copy(table[:, row:row + B, col:col + K],
                                      ps[:, 0:B * K].rearrange("p (b k) -> p b k", b=B)).then_inc(att_in_table, 1)

            def mix_step(s, ahead, layer, k, to, done):
                col = {0: C_ATT0, 1: C_ATT23, 2: C_ATT23 + K}[layer] + k
                nc.vector.scalar_tensor_tensor(out=to[:], in0=mix_sb[:, layer, k, :],
                                               scalar=cur[s.parity(0)][:, col:col + 1],
                                               in1=eye_sb[:] if k == 0 else to[:], op0=ALU.mult,
                                               op1=ALU.add).then_inc(done, 1)

            def mix_a0(s, k):
                if k == 0:
                    wait(dve, l0_done, s.count(G, 0, G))
                else:
                    dve.wait_ge(mixed0, s.count(K, 2, k))
                mix_step(s, 2, 0, k, a0[s.parity(2)], mixed0)

            def mix_a23(s, k):
                if k == 0:
                    wait(dve, m_done, s.count(1, -3, 1))
                else:
                    dve.wait_ge(mixed23, s.count(2 * K, -1, 2 * k))
                mix_step(s, -1, 1, k, a2[s.parity(-1)], mixed23)
                mix_step(s, -1, 2, k, a3[s.parity(-1)], mixed23)

            def slot(s):
                c = cur[s.parity(0)]
                dve.wait_ge(cur_set, s.count(1, 0, 3))
                if s.has(-2):
                    j = s.parity(-2)
                    dve.wait_ge(m_hi_done, s.count(1, -2, 1))
                    wait(dve, y_out, s.count(PH, -4, PH))
                    nc.vector.tensor_tensor(m_lo[j][:], m_ps[:, 0:P], m_hi[j][:].bitcast(F32), ALU.subtract)
                    nc.vector.tensor_tensor(e_col[j][:], m_ps[:, P:P + 1], c[:, C_C3:C_C3 + 1],
                                            ALU.add).then_inc(m_lo_done, 1)
                for g in range(G):
                    if s.has(1):
                        j = s.parity(1)
                        dve.wait_ge(x1_hi_done, s.count(G, 1, g + 1))
                        nc.vector.scalar_tensor_tensor(out=x1_lo[j][:, g, 1:T + 1], in0=l0_ps[g % 2][:, 0:T],
                                                       scalar=c[:, C_C0 + g:C_C0 + g + 1],
                                                       in1=x1_hi[j][:, g, 1:T + 1].bitcast(F32), op0=ALU.add,
                                                       op1=ALU.subtract).then_inc(x1_lo_done, 1)
                    for k in (2 * g, 2 * g + 1):
                        if s.has(2):
                            mix_a0(s, k)
                        if s.has(-1):
                            mix_a23(s, k)

            slots = []
            def first_then_setup(s):
                slot(s)
                if s.known and 2 * s.i + s.r == FIRST:
                    dve.wait_ge(setup_pe, 5)
                    step(nc.vector.tensor_copy(att_t[:], m_ps[0:K, 128:128 + NL * B].rearrange("k (n b) -> k n b", n=NL)))
                    assert steps[0] == ATT_T
                    dve.wait_ge(setup_pe, 6)
                    for ps, row, col, first, n in ((y_ps[0], 1, C_C0, 0, G), (y_ps[1], 2, C_D, 0, G),
                                                   (y_ps[0], 4, C_C2, G, 1), (y_ps[0], 4, C_C3, G + 1, 1)):
                        nc.vector.tensor_copy(
                            table[:, row:row + B, col:col + n].rearrange("p b g -> p g b"),
                            ps[:, B * first:B * (first + n)].rearrange("p (g b) -> p g b", g=n)).then_inc(bias_in_table, 1)
                if s.known and 2 * s.i + s.r == FIRST + 1:
                    dve.wait_ge(conv_loaded, DMA)
                    for g in range(G):
                        step(nc.vector.tensor_tensor(conv_f[:, g, 1, :], conv_f[:, g, 1, :], eye_sb[:], ALU.add))
                    nc.vector.tensor_copy(conv_hi[:], conv_f[:]).then_inc(conv_split, 1)
                    dve.wait_ge(conv_split, 1)
                    nc.vector.tensor_tensor(conv_lo[:], conv_f[:], conv_hi[:].bitcast(F32),
                                            ALU.subtract).then_inc(conv_split, 1)

            run_slots(dve, first_then_setup)


GELU_STEPS = 3 + 3 + 2 + 1 + (len(ERF_P) - 3) + 1 + 1 + (len(ERF_Q) - 3) + 1 + 4
HID0 = 1 + GELU_STEPS
HID1 = HID0 + GELU_STEPS
LSUB = HID1 + 2
DIAG = LSUB + 3 + NL
ATT_T = DIAG + 1

_INS = ["x", "cond_t", "w0", "w1", "w2", "b0", "b1", "b2", "mix", "bias0", "bias2", "bias3", "conv", "c_weight",
        "fside", "eye"]


def kernel(**inputs):
    import numpy as np
    import concourse.bacc as bacc
    from concourse.bass_utils import run_bass_kernel_spmd

    a = {n: np.asarray(v) for n, v in inputs.items()}
    layers = ("L0", "L2", "L3")

    def stack(name, axis):
        return np.stack([a[f"{n}_cond_{name}"] for n in layers], axis=axis)

    taps = a["L1_cond_weight"].reshape(G, CG, CG, TAPS)
    conv = np.zeros((PH, CG, G, SHIFTS, PH, CG), np.float32)
    for s in range(SHIFTS):
        for q in range(PH):
            for p in range(PH):
                k = 4 * (s - 1) + q - p + TAPS // 2
                if 0 <= k < TAPS:
                    conv[q, :, :, s, p, :] = taps[:, :, :, k].transpose(2, 0, 1)

    def by_phase(m):
        m = m.reshape(m.shape[0], G, 1, CG)
        return np.broadcast_to(m, (m.shape[0], G, PH, CG)).reshape(m.shape[0], G, P)

    w = [a[f"{n}_cond_weight"][..., 0] for n in layers]
    laid = {
        "x": a["x"].reshape(B, P, T, PH).transpose(0, 1, 3, 2),
        "cond_t": a["cond_128"].T,
        "w0": stack("W0", 1), "w1": stack("W1", 1), "w2": stack("W2", 1),
        "b0": stack("b0", 1), "b1": stack("b1", 1), "b2": stack("b2", 0).reshape(1, NL * K),
        "mix": np.stack([w[0].transpose(2, 0, 1), w[1].transpose(1, 0, 2), w[2].transpose(2, 0, 1)], axis=1),
        "bias0": by_phase(a["L0_cond_bias_k"]), "bias2": a["L2_cond_bias_k"], "bias3": a["L3_cond_bias_k"],
        "conv": conv.reshape(P, G, SHIFTS, P),
        "c_weight": by_phase(a["L1_cond_c_weight"].T),
        "fside": by_phase(a["fside_S_0"].reshape(1, P)),
        "eye": np.eye(P, dtype=np.float32),
    }
    nc = bacc.Bacc("TRN2", target_bir_lowering=False, num_devices=1)
    arrays, args = {}, []
    for name in _INS:
        v = np.ascontiguousarray(laid[name])
        arrays[f"in_{name}_dram"] = v
        args.append(nc.dram_tensor(f"in_{name}_dram", v.shape, mybir.dt.from_np(v.dtype), kind="ExternalInput").ap())
    args.append(nc.dram_tensor("out_dram", (B, P, PH, T), F32, kind="ExternalOutput").ap())
    cond_resid_kernel(nc, *args)
    got = run_bass_kernel_spmd(nc, [arrays], core_ids=[0]).results[0]["out_dram"]
    return np.ascontiguousarray(got.transpose(0, 1, 3, 2)).reshape(B, P, L)
```

```python
from contextlib import ExitStack

import concourse.bass as bass
from concourse import mybir

F32 = mybir.dt.float32
F32R = mybir.dt.float32r
ALU = mybir.AluOpType
ACT = mybir.ActivationFunctionType
AX_X = mybir.AxisListType.X

P = 128
B = 32
L = 2048
K = 8
PH = 4
G = 4
CG = P // G
T = L // PH
TAPS = 9
SHIFTS = 3
NL = 3
OG = 16
NOG = P // OG
DMA = 16
PAIR = 2
UNITS = B // PAIR * PH

X_LOAD, X_SPLIT, LAYER0, X1_SPLIT, CONV, X2_SPLIT, OUTPUT, STORE = 8, 7, 6, 1, 0, -5, -6, -7
FIRST, LAST = -X_LOAD, UNITS - 1 - STORE
BODY = 8
LOOP_FROM, LOOP_TO = 2 * BODY, UNITS - BODY - 1

C_C0, C_D, C_E = 0, 4, 12
COLS = 16

N_COND, N_W0, N_B0, N_B1 = 0, B, B + NL * P, B + NL * P + NL
N_W1 = N_B1 + NL
N_W2 = N_W1 + NL * P
NET_COLS = N_W2 + NL * K


class Step:

    def __init__(self, i, r):
        self.i, self.r = i, r
        self.known = isinstance(i, int)
        self.u = BODY * i + r if self.known else None

    def has(self, lead):
        return not self.known or 0 <= self.u + lead < UNITS

    def is_first(self, lead, unit=0):
        return self.known and self.u + lead == unit

    def quarter(self, lead):
        return (self.r + lead) % PH

    def side(self, lead):
        return (self.r + lead) % 2

    def pair_side(self, lead):
        return (self.r + lead) // PH % 2

    def count(self, per, lead, extra=0):
        return self.i * (BODY * per) + (per * (self.r + lead) + extra)

    def uses(self, per, lead, extra=0):
        return self.i * (BODY // 2 * per) + (per * ((self.r + lead) // 2) + extra)

    def pairs(self, per, lead, extra=0):
        return self.i * (BODY // PH * per) + (per * ((self.r + lead) // PH) + extra)


def wait(eng, semaphore, value):
    if not isinstance(value, int) or value > 0:
        eng.wait_ge(semaphore, value)


def share(s, total, first, end):
    if not s.known or not first <= s.u < end:
        return range(0)
    return range(total * (s.u - first) // (end - first), total * (s.u + 1 - first) // (end - first))


def mixes_of(s):
    return [NOG + n for n in share(s, (NL - 1) * NOG, -LAYER0, -LAYER0 // 2)]


def pairs_of(s):
    return share(s, B // PAIR, -LAYER0 // 2, 0)


def run_steps(eng, body, first=FIRST):
    for u in range(first, LOOP_FROM):
        body(Step(u // BODY, u % BODY))
    with eng.Fori(LOOP_FROM // BODY, (LOOP_TO + 1) // BODY) as i:
        for r in range(BODY):
            body(Step(i, r))
    for u in range(LOOP_TO + 1, LAST + 1):
        body(Step(u // BODY, u % BODY))


def cond_resid_kernel(nc, x, net, rows, consts, mix, bias, conv, c_weight, out):
    with ExitStack() as ctx:
        def sb(name, shape, dt=F32):
            return ctx.enter_context(nc.sbuf_tensor(name, shape, dt))

        def sem(name):
            return ctx.enter_context(nc.semaphore(name))

        def two(name, shape, dt=F32):
            return [sb(f"{name}{j}", shape, dt) for j in range(2)]

        x_sb = two("x_sb", [P, PAIR, T])
        x_hi = two("x_hi", [P, PAIR, T], F32R)
        x_lo = two("x_lo", [P, PAIR, T], F32R)
        x1_chan = two("x1_chan", [P, PAIR, T])
        x1_poly = two("x1_poly", [P, G, PAIR, T])
        x1_hi = two("x1_hi", [P, PAIR, T + 2], F32R)
        x1_lo = two("x1_lo", [P, PAIR, T + 2], F32R)
        x2_poly = two("x2_poly", [P, PAIR, T])
        x2_chan = two("x2_chan", [P, PH, PAIR, T])
        x2_hi = two("x2_hi", [P, PAIR, T], F32R)
        x2_lo = two("x2_lo", [P, PAIR, T], F32R)
        y_sb = two("y_sb", [P, PAIR, T])
        a0_hi = two("a0_hi", [P, PAIR, P], F32R)
        a0_lo = two("a0_lo", [P, PAIR, P], F32R)
        m_hi = two("m_hi", [P, PAIR, P], F32R)
        m_lo = two("m_lo", [P, PAIR, P], F32R)
        cur = two("cur", [P, COLS])
        a0_all = sb("a0_all", [P, B, P])
        m_all = sb("m_all", [P, B, P])
        conv_hi = sb("conv_hi", [P, G, SHIFTS, P], F32R)
        conv_lo = sb("conv_lo", [P, G, SHIFTS, P], F32R)
        c0_all = sb("c0_all", [P, B + PAIR])
        c2_all = sb("c2_all", [P, B])
        c3_all = sb("c3_all", [P, B])
        d_all = sb("d_all", [P, B, G])
        e_all = sb("e_all", [P, B])
        consts_sb = sb("consts_sb", [P, P + OG])
        eye_sb, mask_sb = consts_sb[:, 0:P], consts_sb[:, P:P + OG]
        rows_sb = sb("rows_sb", [1, NL * K + G * P])
        b2_row, fside_row = rows_sb[:, 0:NL * K], rows_sb[:, NL * K:].rearrange("p (g m) -> p g m", g=G)
        bias_sb = sb("bias_sb", [K, NL, P])
        ones_sb = sb("ones_sb", [1, B])
        hid0 = sb("hid0", [P, NL, B])
        hid1 = sb("hid1", [P, NL, B])
        lmax = sb("lmax", [B, NL])
        lsub = sb("lsub", [B, NL, K])
        lexp = sb("lexp", [B, NL, K])
        lsum = sb("lsum", [B, NL])
        linv = sb("linv", [B, NL])
        att = sb("att", [B, NL, K, OG])
        att_hi = sb("att_hi", [P, NL, B], F32R)
        att_lo = sb("att_lo", [P, NL, B])
        att_t = sb("att_t", [K, NL, B])

        def part(buf, pattern, at, size):
            return buf[:].rearrange(pattern)[:, at:at + size]

        late = (x1_poly[1], "p g b t -> p (g b t)")
        conv_f = part(*late, 0, G * SHIFTS * P).rearrange("p (g s m) -> p g s m", g=G, s=SHIFTS)
        cw_sb = part(*late, 1536, G * P).rearrange("p (g m) -> p g m", g=G)

        def halves(hi, lo, at):
            return [b[:, at:at + B * OG].rearrange("p (b o) -> p b o", b=B) for b in (hi, lo)]

        flat = "p b t -> p (b t)"
        spare = [buf[1][:].rearrange(flat) for buf in (x1_hi, x1_lo)]
        after_a0 = [buf[0][:].rearrange(flat) for buf in (x1_hi, x1_lo)]
        spread = [halves(*spare, 0), halves(*spare, B * OG), halves(*after_a0, 0)]

        def by_og(buf):
            return part(buf, flat, 0, NOG * P).rearrange("p (g m) -> p g m", g=NOG)

        mix_f = [by_og(y_sb[0]), by_og(x2_poly[0]), by_og(x2_poly[1])]
        mix_parts = [(by_og(x1_hi[0]), by_og(x1_lo[0])), (by_og(x2_hi[0]), by_og(x2_lo[0])),
                     (by_og(x2_hi[1]), by_og(x2_lo[1]))]
        net_sb = part(y_sb[1], flat, 0, NET_COLS)
        cond_sb = net_sb[:, N_COND:N_COND + B]
        w0_sb = net_sb[:, N_W0:N_W0 + NL * P].rearrange("p (n m) -> p n m", n=NL)
        w1_sb = net_sb[:, N_W1:N_W1 + NL * P].rearrange("p (n m) -> p n m", n=NL)
        w2_sb = net_sb[:, N_W2:N_W2 + NL * K].rearrange("p (n k) -> p n k", n=NL)
        b0_sb, b1_sb = net_sb[:, N_B0:N_B0 + NL], net_sb[:, N_B1:N_B1 + NL]
        a23_all = [buf[:].rearrange("p q b t -> p (q b t)").rearrange("p (n m) -> p n m", n=B)
                   for buf in x2_chan]

        def banks(name):
            return ctx.enter_context(nc.psum_tensor(name, [P, PAIR, 512], F32))

        l0_ps = banks("l0_ps")
        cv_ps = banks("cv_ps")
        y_ps = banks("y_ps")
        mix_ps = banks("mix_ps")

        net_loaded = sem("net_loaded")
        net2_loaded = sem("net2_loaded")
        consts_loaded = sem("consts_loaded")
        mix_loaded = [sem(f"mix_loaded{n}") for n in range(NL)]
        bias_loaded = sem("bias_loaded")
        conv_loaded = sem("conv_loaded")
        x_loaded = [sem(f"x_loaded{j}") for j in range(2)]
        remap1 = [sem(f"remap1_{j}") for j in range(2)]
        remap2 = [sem(f"remap2_{j}") for j in range(2)]
        stored = [sem(f"stored{j}") for j in range(2)]
        ones_set = sem("ones_set")
        chain = sem("chain")
        pool_chain = sem("pool_chain")
        gelus = sem("gelus")
        logits_less_max = sem("logits_less_max")
        att_ready = sem("att_ready")
        att_split = sem("att_split")
        att_t_ready = sem("att_t_ready")
        spread_hi = [sem(f"spread_hi{n}") for n in range(NL)]
        spread_lo = [sem(f"spread_lo{n}") for n in range(NL)]
        mix_split = [sem(f"mix_split{n}") for n in range(NL)]
        setup_pe = sem("setup_pe")
        exp_done = sem("exp_done")
        mix_made = sem("mix_made")
        mix_out = sem("mix_out")
        bias_out = sem("bias_out")
        m_made = sem("m_made")
        m_out = sem("m_out")
        e_out = sem("e_out")
        zero_cols = sem("zero_cols")
        zero_consts = sem("zero_consts")
        conv_split = sem("conv_split")
        cur_set = sem("cur_set")
        a0_split = sem("a0_split")
        m_split = sem("m_split")
        x_hi_done = sem("x_hi_done")
        x_lo_done = sem("x_lo_done")
        l0_done = sem("l0_done")
        x1_out = sem("x1_out")
        x1_hi_done = sem("x1_hi_done")
        x1_lo_done = sem("x1_lo_done")
        conv_done = sem("conv_done")
        x2_out = sem("x2_out")
        x2_hi_done = sem("x2_hi_done")
        x2_lo_done = sem("x2_lo_done")
        y_done = sem("y_done")
        y_out = sem("y_out")
        ROWS_DMA = 4 * DMA

        prep_ps = [mix_ps[:, 0, :], mix_ps[:, 1, :], cv_ps[:, 0, :], cv_ps[:, 1, :]]
        RING = len(prep_ps)

        block = ctx.enter_context(nc.Block())

        @block.sync
        def _(sp):
            def load(s):
                wait(sp, x_lo_done, s.count(1, X_LOAD, -1))
                sp.dma_start(x_sb[s.side(X_LOAD)][:],
                             x[bass.ds(s.pairs(PAIR, X_LOAD), PAIR), :, s.quarter(X_LOAD), :].rearrange(
                                 "b c t -> c b t")).then_inc(x_loaded[s.side(X_LOAD)], DMA)

            sp.dma_start(net_sb[:, :N_W1], net[:, :N_W1]).then_inc(net_loaded, DMA)
            sp.dma_start(net_sb[:, N_W1:], net[:, N_W1:]).then_inc(net2_loaded, DMA)
            sp.dma_start(rows_sb[:], rows).then_inc(net2_loaded, DMA)
            sp.dma_start(consts_sb[:], consts).then_inc(consts_loaded, DMA)
            sp.dma_start(mix_f[0], mix[:, 0]).then_inc(mix_loaded[0], DMA)
            load(Step(-1, 0))
            sp.dma_start(bias_sb[:], bias).then_inc(bias_loaded, DMA)
            sp.dma_start(cw_sb, c_weight).then_inc(bias_loaded, DMA)
            for n in range(1, NL):
                sp.dma_start(mix_f[n], mix[:, n]).then_inc(mix_loaded[n], DMA)
            sp.dma_start(conv_f, conv).then_inc(conv_loaded, DMA)

            def step(s):
                if s.has(X_LOAD):
                    load(s)
                if s.has(LAYER0):
                    q, j = s.quarter(LAYER0), s.side(LAYER0)
                    wait(sp, x1_out, s.count(2, LAYER0, 2))
                    for g in range(G):
                        sp.dma_start(x1_poly[s.pair_side(LAYER0)][CG * q:CG * (q + 1), g],
                                     x1_chan[j][CG * g:CG * (g + 1)]).then_inc(remap1[j], DMA)
                if s.has(STORE):
                    wait(sp, y_out, s.count(2, STORE, 2))
                    sp.dma_start(out[bass.ds(s.pairs(PAIR, STORE), PAIR), :, s.quarter(STORE), :].rearrange(
                        "b c t -> c b t"), y_sb[s.side(STORE)][:]).then_inc(stored[s.side(STORE)], DMA)
                if s.has(CONV):
                    g, j = s.quarter(CONV), s.side(CONV)
                    wait(sp, x2_out, s.count(2, CONV, 2))
                    for p in range(PH):
                        sp.dma_start(x2_chan[s.pair_side(CONV)][CG * g:CG * (g + 1), p],
                                     x2_poly[j][CG * p:CG * (p + 1)]).then_inc(remap2[j], DMA)

            run_steps(sp, step, FIRST + 1)
            for j in range(2):
                sp.wait_ge(stored[j], DMA * (UNITS // 2))

        @block.tensor
        def _(pe):
            pe.wait_ge(net_loaded, DMA)
            for n in range(NL):
                pe.matmul(y_ps[:, 0, B * n:B * (n + 1)], w0_sb[:, n, :], cond_sb, start=True,
                          stop=True).then_inc(setup_pe, 1)
            pe.wait_ge(net2_loaded, 2 * DMA)
            for n in range(NL):
                pe.wait_ge(gelus, n + 1)
                pe.matmul(y_ps[:, 1, B * n:B * (n + 1)], w1_sb[:, n, :], hid0[:, n, :], start=True,
                          stop=True).then_inc(setup_pe, 1)
            logits = y_ps[0:B, 0, 128:128 + NL * K]
            pe.wait_ge(ones_set, 1)
            pe.matmul(logits, ones_sb[:], b2_row, start=True, stop=False, skip_group_check=True)
            for n in range(NL):
                pe.wait_ge(gelus, NL + n + 1)
                mm = pe.matmul(logits[:, K * n:K * (n + 1)], hid1[:, n, :], w2_sb[:, n, :], start=False, stop=True,
                               skip_group_check=True)
            mm.then_inc(setup_pe, 1)
            pe.wait_ge(consts_loaded, DMA)
            pe.wait_ge(att_ready, 1)
            for n in range(NL):
                mm = pe.matmul(l0_ps[:, 0, B * n:B * (n + 1)], att[:, n].rearrange("b k o -> b (k o)"),
                               eye_sb[0:B, 0:B], start=True, stop=True)
            mm.then_inc(setup_pe, 1)
            for n in range(NL):
                mm = pe.matmul(l0_ps[0:K, 1, B * n:B * (n + 1)], att[:, n, :, 0], eye_sb[0:B, 0:B], start=True,
                               stop=True)
            mm.then_inc(setup_pe, 1)

            def mixture(n):
                layer, o = n // NOG, n % NOG
                if o == 0:
                    pe.wait_ge(mix_split[layer], 2)
                    pe.wait_ge(spread_hi[layer], 1)
                    pe.wait_ge(spread_lo[layer], 1)
                wait(pe, mix_out, n + 1 - RING)
                (w_hi, w_lo), (a_hi, a_lo) = mix_parts[layer], spread[layer]
                for k, (w, a) in enumerate(((w_hi, a_hi), (w_lo, a_hi), (w_hi, a_lo))):
                    mm = pe.matmul(prep_ps[n % RING], w[:, o, :], a.rearrange("p b o -> p (b o)"), start=(k == 0),
                                   stop=(k == 2))
                mm.then_inc(mix_made, 1)

            def pair_product(m):
                if m == 0:
                    pe.wait_ge(mix_out, NL * NOG)
                    pe.wait_ge(bias_out, 4)
                wait(pe, m_out, m + 1 - RING)
                wait(pe, e_out, m + 1 - RING)
                ps = prep_ps[m % RING]
                for k in range(PAIR):
                    n = PAIR * m + k
                    pe.matmul(ps[:, P * k:P * (k + 1)], a23_all[0][:, n, :], a23_all[1][:, n, :],
                              start=True, stop=True)
                    mm = pe.matmul(ps[:, PAIR * P + k:PAIR * P + k + 1], a23_all[1][:, n, :], c2_all[:, n:n + 1],
                                   start=True, stop=True)
                mm.then_inc(m_made, 1)

            def biases():
                pe.wait_ge(bias_loaded, 2 * DMA)
                for g in range(G):
                    pe.matmul(y_ps[:, 1, 128 + B * g:128 + B * (g + 1)], cw_sb[:, g, :], cond_sb, start=True,
                              stop=False)
                    pe.matmul(y_ps[:, 1, 128 + B * g:128 + B * (g + 1)], fside_row[:, g, :], ones_sb[:],
                              start=False, stop=True)
                pe.wait_ge(att_t_ready, 1)
                for n in range(NL):
                    mm = pe.matmul(y_ps[:, 0, 256 + B * n:256 + B * (n + 1)], bias_sb[:, n, :], att_t[:, n, :],
                                   start=True, stop=True)
                mm.then_inc(setup_pe, 1)

            for n in range(NOG):
                mixture(n)
            biases()

            def layer0(s):
                pe.wait_ge(x_lo_done, s.count(1, LAYER0, 1))
                if s.quarter(LAYER0) == 0:
                    pe.wait_ge(a0_split, s.pairs(2, LAYER0, 2))
                if s.is_first(LAYER0):
                    pe.wait_ge(att_split, 2)
                    pe.wait_ge(att_t_ready, 1)
                j, m = s.side(LAYER0), s.pair_side(LAYER0)
                for k in range(PAIR):
                    wait(pe, x1_out, s.count(2, LAYER0, k - 1))
                    for n, (w, a) in enumerate(((a0_hi, x_hi), (a0_lo, x_hi), (a0_hi, x_lo))):
                        mm = pe.matmul(l0_ps[:, k, 0:T], w[m][:, k, :], a[j][:, k, :], start=(n == 0), stop=(n == 2))
                    mm.then_inc(l0_done, 1)

            def convolve(s):
                pe.wait_ge(x1_lo_done, s.count(1, CONV, 1))
                if s.is_first(CONV):
                    pe.wait_ge(conv_split, 2)
                    pe.wait_ge(zero_cols, 4)
                    pe.wait_ge(m_out, B // PAIR)
                    pe.wait_ge(e_out, B // PAIR)
                j, g = s.side(CONV), s.quarter(CONV)
                for k in range(PAIR):
                    wait(pe, x2_out, s.count(2, CONV, k - 1))
                    n = 0
                    for sh in range(SHIFTS):
                        for w, a in ((conv_hi, x1_hi), (conv_lo, x1_hi), (conv_hi, x1_lo)):
                            mm = pe.matmul(cv_ps[:, k, 0:T], w[:, g, sh, :], a[j][:, k, sh:sh + T],
                                           start=(n == 0), stop=(n == 3 * SHIFTS - 1))
                            n += 1
                    mm.then_inc(conv_done, 1)

            def output(s):
                pe.wait_ge(x2_lo_done, s.count(1, OUTPUT, 1))
                if s.quarter(OUTPUT) == 0:
                    pe.wait_ge(m_split, s.pairs(2, OUTPUT, 2))
                j, m = s.side(OUTPUT), s.pair_side(OUTPUT)
                for k in range(PAIR):
                    wait(pe, y_out, s.count(2, OUTPUT, k - 1))
                    for n, (w, a) in enumerate(((m_hi, x2_hi), (m_lo, x2_hi), (m_hi, x2_lo))):
                        mm = pe.matmul(y_ps[:, k, 0:T], w[m][:, k, :], a[j][:, k, :], start=(n == 0), stop=(n == 2))
                    mm.then_inc(y_done, 1)

            def step(s):
                if s.has(LAYER0):
                    layer0(s)
                if s.has(CONV):
                    convolve(s)
                if s.has(OUTPUT):
                    output(s)
                for n in mixes_of(s):
                    mixture(n)
                for m in pairs_of(s):
                    pair_product(m)

            run_steps(pe, step)

        @block.scalar
        def _(act):
            for layer, (bias, to) in enumerate(((b0_sb, hid0), (b1_sb, hid1))):
                act.wait_ge(setup_pe, NL * (layer + 1))
                for n in range(NL):
                    nc.scalar.activation(to[:, n, :], y_ps[:, layer, B * n:B * (n + 1)], ACT.Gelu,
                                         bias=bias[:, n:n + 1]).then_inc(gelus, 1)
            act.wait_ge(logits_less_max, 1)
            nc.scalar.activation(lexp[:], lsub[:], ACT.Exp).then_inc(exp_done, 1)
            for n in range(1, NL):
                act.wait_ge(mix_loaded[n], DMA)
                nc.scalar.activation(mix_parts[n][0], mix_f[n], ACT.Identity).then_inc(mix_split[n], 1)

            def step(s):
                c = cur[s.pair_side(0)]
                if s.r % PH == 0 or s.is_first(LAYER0):
                    act.wait_ge(cur_set, s.pairs(3, 0, 3 * 3))
                if s.has(LAYER0):
                    j = s.side(LAYER0)
                    wait(act, remap1[j], s.uses(ROWS_DMA, LAYER0))
                    if s.quarter(LAYER0) == 0:
                        wait(act, x1_lo_done, s.count(1, LAYER0, -PH))
                    if s.is_first(LAYER0, PH):
                        act.wait_ge(conv_split, 2)
                        act.wait_ge(mix_made, NL * NOG)
                    for k in range(PAIR):
                        act.wait_ge(l0_done, s.count(2, LAYER0, k + 1))
                        col = C_C0 + PAIR * (((s.r % PH) + LAYER0) // PH - 1) + k
                        nc.scalar.activation(x1_chan[j][:, k, :], l0_ps[:, k, 0:T], ACT.Identity,
                                             bias=c[:, col:col + 1]).then_inc(x1_out, 1)
                if s.has(X2_SPLIT):
                    j, m, p = s.side(X2_SPLIT), s.pair_side(X2_SPLIT), s.quarter(X2_SPLIT)
                    if p == 0:
                        for h in range(2):
                            act.wait_ge(remap2[h], s.uses(ROWS_DMA, X2_SPLIT, 2 * ROWS_DMA))
                    wait(act, y_done, s.count(2, X2_SPLIT, -2))
                    nc.scalar.activation(x2_hi[j][:], x2_chan[m][:, p], ACT.Identity).then_inc(x2_hi_done, 1)
                if s.has(CONV):
                    j = s.side(CONV)
                    wait(act, remap2[j], s.uses(ROWS_DMA, CONV))
                    if s.quarter(CONV) == 0:
                        wait(act, x2_lo_done, s.count(1, CONV, -PH))
                    if s.is_first(CONV):
                        act.wait_ge(m_made, B // PAIR)
                    for k in range(PAIR):
                        act.wait_ge(conv_done, s.count(2, CONV, k + 1))
                        col = C_D + G * k + s.quarter(CONV)
                        nc.scalar.activation(x2_poly[j][:, k, :], cv_ps[:, k, 0:T], ACT.Identity,
                                             bias=c[:, col:col + 1]).then_inc(x2_out, 1)
                if s.has(OUTPUT):
                    j = s.side(OUTPUT)
                    wait(act, stored[j], s.uses(DMA, OUTPUT))
                    for k in range(PAIR):
                        act.wait_ge(y_done, s.count(2, OUTPUT, k + 1))
                        col = C_E + PAIR * (((s.r % PH) + OUTPUT) // PH + 2) + k
                        nc.scalar.activation(y_sb[j][:, k, :], y_ps[:, k, 0:T], ACT.Identity,
                                             bias=c[:, col:col + 1]).then_inc(y_out, 1)
                for m in pairs_of(s):
                    act.wait_ge(m_made, m + 1)
                    nc.scalar.activation(m_all[:, PAIR * m:PAIR * (m + 1), :].rearrange("p n m -> p (n m)"),
                                         prep_ps[m % RING][:, 0:PAIR * P], ACT.Identity).then_inc(m_out, 1)

            run_steps(act, step)

        @block.gpsimd
        def _(pool):
            nc.gpsimd.memset(ones_sb[:], 1.0).then_inc(ones_set, 1)
            for j in range(2):
                nc.gpsimd.memset(cur[j][:], 0.0).then_inc(zero_consts, 1)
            nc.gpsimd.memset(c0_all[:, B:], 0.0).then_inc(zero_consts, 1)

            def spread_part(layer, half):
                src = (att_hi[:].bitcast(F32), att_lo[:])[half][:, layer, :]
                nc.gpsimd.tensor_tensor(spread[layer][half], src.unsqueeze(2).to_broadcast([P, B, OG]),
                                        mask_sb.unsqueeze(1).to_broadcast([P, B, OG]),
                                        ALU.mult).then_inc((spread_hi, spread_lo)[half][layer], 1)

            pool.wait_ge(consts_loaded, DMA)
            pool.wait_ge(att_split, 2)
            spread_part(0, 1)
            for n in range(1, NL):
                if n == NL - 1:
                    pool.wait_ge(mix_made, NOG)
                spread_part(n, 0)
                spread_part(n, 1)
                pool.wait_ge(mix_loaded[n], DMA)
                pool.wait_ge(mix_split[n], 1)
                nc.gpsimd.tensor_tensor(mix_parts[n][1], mix_f[n], mix_parts[n][0].bitcast(F32),
                                        ALU.subtract).then_inc(mix_split[n], 1)
            pool.wait_ge(zero_consts, 3)
            pool.wait_ge(bias_out, 4)

            def set_cur(s):
                to = cur[s.pair_side(0)]
                base = s.pairs(PAIR, 0)
                for table, col, ahead, width, per in ((c0_all, C_C0, PAIR, 2 * PAIR, 1), (d_all, C_D, 0, PAIR, G),
                                                      (e_all, C_E, -2 * PAIR, 2 * PAIR, 1)):
                    lo, hi = 0, width
                    if s.known:
                        lo, hi = max(0, -(base + ahead)), min(width, B - (base + ahead))
                    if lo >= hi:
                        nc.gpsimd.memset(to[:, col:col + 1], 0.0).then_inc(cur_set, 1)
                        continue
                    src = table[:, bass.ds(base + (ahead + lo), hi - lo)]
                    dst = to[:, col + per * lo:col + per * hi]
                    if per > 1:
                        dst = dst.rearrange("p (n g) -> p n g", g=per)
                    nc.gpsimd.tensor_copy(dst, src).then_inc(cur_set, 1)

            def step(s):
                if s.is_first(X_SPLIT):
                    pool.wait_ge(conv_loaded, DMA)
                    nc.gpsimd.tensor_tensor(conv_f[:, :, 1, :], conv_f[:, :, 1, :],
                                            eye_sb.unsqueeze(1).to_broadcast([P, G, P]), ALU.add).then_inc(pool_chain, 1)
                    pool.wait_ge(pool_chain, 1)
                    nc.gpsimd.tensor_copy(conv_hi[:], conv_f).then_inc(conv_split, 1)
                    pool.wait_ge(conv_split, 1)
                    nc.gpsimd.tensor_tensor(conv_lo[:], conv_f, conv_hi[:].bitcast(F32),
                                            ALU.subtract).then_inc(conv_split, 1)
                    pool.wait_ge(mix_made, NL * NOG)
                    for j in range(2):
                        for buf in (x1_hi[j], x1_lo[j]):
                            nc.gpsimd.memset(buf[:, :, 0:T + 2:T + 1].bitcast(F32), 0.0).then_inc(zero_cols, 1)
                if s.r % PH:
                    return
                ahead = Step(s.i, s.r + PH) if not s.known else Step((s.u + PH) // BODY, (s.u + PH) % BODY)
                if s.known and s.u + PH > LAST:
                    return
                if s.is_first(0):
                    pool.wait_ge(e_out, B // PAIR)
                if not s.known:
                    pool.wait_ge(x1_out, s.count(2, LAYER0, 0))
                    pool.wait_ge(x2_out, s.count(2, CONV, 0))
                    pool.wait_ge(y_out, s.count(2, OUTPUT, 0))
                else:
                    for done, lead in ((x1_out, LAYER0), (x2_out, CONV), (y_out, OUTPUT)):
                        wait(pool, done, 2 * min(s.u + lead, UNITS))
                set_cur(ahead)

            set_cur(Step(-1, 0))
            run_steps(pool, step, -BODY)

        @block.vector
        def _(dve):
            steps = [0]

            def after(ins):
                steps[0] += 1
                ins.then_inc(chain, 1)
                dve.wait_ge(chain, steps[0])

            def mix_evacuate(n):
                layer, o = n // NOG, n % NOG
                to = a0_all if layer == 0 else a23_all[layer - 1]
                dve.wait_ge(mix_made, n + 1)
                nc.vector.tensor_tensor(to[:, :, OG * o:OG * (o + 1)],
                                        prep_ps[n % RING].rearrange("p (b o) -> p b o", b=B),
                                        eye_sb[:, OG * o:OG * (o + 1)].unsqueeze(1).to_broadcast([P, B, OG]),
                                        ALU.add).then_inc(mix_out, 1)

            def split_x(s):
                j = s.side(X_SPLIT)
                dve.wait_ge(x_loaded[j], s.uses(DMA, X_SPLIT, DMA))
                wait(dve, l0_done, s.count(2, X_SPLIT, -2))
                nc.vector.tensor_copy(x_hi[j][:], x_sb[j][:]).then_inc(x_hi_done, 1)
                dve.wait_ge(x_hi_done, s.count(1, X_SPLIT, 1))
                nc.vector.tensor_tensor(x_lo[j][:], x_sb[j][:], x_hi[j][:].bitcast(F32),
                                        ALU.subtract).then_inc(x_lo_done, 1)

            def split_weights(s, lead, every, hi, lo, done, reader):
                m = s.pair_side(lead)
                src = every[:, bass.ds(s.pairs(PAIR, lead), PAIR), :]
                wait(dve, reader, s.count(2, lead, -2 * PH))
                nc.vector.tensor_scalar(hi[m][:], src, 1.0, None, ALU.mult).then_inc(done, 1)
                dve.wait_ge(done, s.pairs(2, lead, 1))
                nc.vector.tensor_tensor(lo[m][:], src, hi[m][:].bitcast(F32), ALU.subtract).then_inc(done, 1)

            def step(s):
                if s.has(X1_SPLIT):
                    j, m, g = s.side(X1_SPLIT), s.pair_side(X1_SPLIT), s.quarter(X1_SPLIT)
                    if g == 0:
                        for h in range(2):
                            dve.wait_ge(remap1[h], s.uses(ROWS_DMA, X1_SPLIT, 2 * ROWS_DMA))
                    wait(dve, conv_done, s.count(2, X1_SPLIT, -2))
                    nc.vector.tensor_copy(x1_hi[j][:, :, 1:T + 1], x1_poly[m][:, g]).then_inc(x1_hi_done, 1)
                    dve.wait_ge(x1_hi_done, s.count(1, X1_SPLIT, 1))
                    nc.vector.tensor_tensor(x1_lo[j][:, :, 1:T + 1], x1_poly[m][:, g],
                                            x1_hi[j][:, :, 1:T + 1].bitcast(F32), ALU.subtract).then_inc(x1_lo_done, 1)
                if s.has(X_SPLIT):
                    if not s.is_first(X_SPLIT):
                        split_x(s)
                    if s.quarter(X_SPLIT) == 0:
                        split_weights(s, X_SPLIT, a0_all, a0_hi, a0_lo, a0_split, l0_done)
                if s.has(X2_SPLIT):
                    j, m, p = s.side(X2_SPLIT), s.pair_side(X2_SPLIT), s.quarter(X2_SPLIT)
                    if p == 0:
                        if s.is_first(X2_SPLIT):
                            dve.wait_ge(m_out, B // PAIR)
                        split_weights(s, X2_SPLIT, m_all, m_hi, m_lo, m_split, y_done)
                        for h in range(2):
                            dve.wait_ge(remap2[h], s.uses(ROWS_DMA, X2_SPLIT, 2 * ROWS_DMA))
                    dve.wait_ge(x2_hi_done, s.count(1, X2_SPLIT, 1))
                    wait(dve, y_done, s.count(2, X2_SPLIT, -2))
                    nc.vector.tensor_tensor(x2_lo[j][:], x2_chan[m][:, p], x2_hi[j][:].bitcast(F32),
                                            ALU.subtract).then_inc(x2_lo_done, 1)
                for n in mixes_of(s):
                    mix_evacuate(n)
                for m in pairs_of(s):
                    dve.wait_ge(m_out, m + 1)
                    nc.vector.tensor_tensor(e_all[:, PAIR * m:PAIR * (m + 1)],
                                            prep_ps[m % RING][:, PAIR * P:PAIR * (P + 1)],
                                            c3_all[:, PAIR * m:PAIR * (m + 1)], ALU.add).then_inc(e_out, 1)

            dve.wait_ge(mix_loaded[0], DMA)
            nc.vector.tensor_copy(mix_parts[0][0], mix_f[0]).then_inc(mix_split[0], 1)
            dve.wait_ge(mix_split[0], 1)
            nc.vector.tensor_tensor(mix_parts[0][1], mix_f[0], mix_parts[0][0].bitcast(F32),
                                    ALU.subtract).then_inc(mix_split[0], 1)
            dve.wait_ge(setup_pe, 2 * NL + 1)
            logits = y_ps[0:B, 0, 128:128 + NL * K].rearrange("b (n k) -> b n k", n=NL)
            after(nc.vector.tensor_reduce(lmax[:], logits, AX_X, ALU.max))
            nc.vector.tensor_tensor(lsub[:], logits, lmax[:].unsqueeze(2).to_broadcast([B, NL, K]),
                                    ALU.subtract).then_inc(logits_less_max, 1)
            dve.wait_ge(exp_done, 1)
            after(nc.vector.tensor_reduce(lsum[:], lexp[:], AX_X, ALU.add))
            after(nc.vector.reciprocal(linv[:], lsum[:]))
            nc.vector.tensor_tensor(att[:], lexp[:].unsqueeze(3).to_broadcast([B, NL, K, OG]),
                                    linv[:].unsqueeze(2).unsqueeze(3).to_broadcast([B, NL, K, OG]),
                                    ALU.mult).then_inc(att_ready, 1)
            dve.wait_ge(consts_loaded, DMA)
            dve.wait_ge(setup_pe, 2 * NL + 2)
            att_ps = l0_ps[:, 0, 0:NL * B].rearrange("p (n b) -> p n b", n=NL)
            nc.vector.tensor_copy(att_hi[:], att_ps).then_inc(att_split, 1)
            dve.wait_ge(att_split, 1)
            nc.vector.tensor_tensor(att_lo[:], att_ps, att_hi[:].bitcast(F32), ALU.subtract).then_inc(att_split, 1)
            nc.vector.tensor_tensor(spread[0][0], att_hi[:, 0, :].bitcast(F32).unsqueeze(2).to_broadcast([P, B, OG]),
                                    mask_sb.unsqueeze(1).to_broadcast([P, B, OG]), ALU.mult).then_inc(spread_hi[0], 1)
            dve.wait_ge(setup_pe, 2 * NL + 3)
            nc.vector.tensor_copy(att_t[:], l0_ps[0:K, 1, 0:NL * B].rearrange("k (n b) -> k n b",
                                                                              n=NL)).then_inc(att_t_ready, 1)
            for n in range(NOG):
                mix_evacuate(n)
            split_x(Step(-1, BODY - X_SPLIT))
            dve.wait_ge(setup_pe, 2 * NL + 4)
            for n, to in enumerate((c0_all, c2_all, c3_all)):
                nc.vector.tensor_copy(to[:, 0:B], y_ps[:, 0, 256 + B * n:256 + B * (n + 1)]).then_inc(bias_out, 1)
            nc.vector.tensor_copy(d_all[:].rearrange("p n g -> p g n"),
                                  y_ps[:, 1, 128:128 + G * B].rearrange("p (g n) -> p g n", g=G)).then_inc(bias_out, 1)
            dve.wait_ge(mix_out, NOG)
            run_steps(dve, step, -X_SPLIT)


_INS = ["x", "net", "rows", "consts", "mix", "bias", "conv", "c_weight"]


def kernel(**inputs):
    import numpy as np
    import concourse.bacc as bacc
    from concourse.bass_utils import run_bass_kernel_spmd

    a = {n: np.asarray(v) for n, v in inputs.items()}
    layers = ("L0", "L2", "L3")

    def stack(name, axis):
        return np.stack([a[f"{n}_cond_{name}"] for n in layers], axis=axis)

    taps = a["L1_cond_weight"].reshape(G, CG, CG, TAPS)
    conv = np.zeros((PH, CG, G, SHIFTS, PH, CG), np.float32)
    for s in range(SHIFTS):
        for q in range(PH):
            for p in range(PH):
                k = PH * (s - 1) + q - p + TAPS // 2
                if 0 <= k < TAPS:
                    conv[q, :, :, s, p, :] = taps[:, :, :, k].transpose(2, 0, 1)

    def by_phase(m):
        m = m.reshape(m.shape[0], G, 1, CG)
        return np.broadcast_to(m, (m.shape[0], G, PH, CG)).reshape(m.shape[0], G, P)

    def by_columns(m):
        return m.reshape(K, NOG, OG, P).transpose(0, 2, 1, 3).reshape(K * OG, NOG, P)

    w = [a[f"{n}_cond_weight"][..., 0] for n in layers]
    laid = {
        "x": a["x"].reshape(B, P, T, PH).transpose(0, 1, 3, 2),
        "net": np.concatenate([a["cond_128"].T, stack("W0", 1).reshape(P, NL * P), stack("b0", 1), stack("b1", 1),
                               stack("W1", 1).reshape(P, NL * P), stack("W2", 1).reshape(P, NL * K)], axis=1),
        "rows": np.concatenate([stack("b2", 0).reshape(1, NL * K), by_phase(a["fside_S_0"].reshape(1, P)).reshape(1, -1)],
                               axis=1),
        "consts": np.concatenate([np.eye(P, dtype=np.float32), np.tile(np.eye(OG, dtype=np.float32), (K, 1))],
                                 axis=1),
        "mix": np.stack([by_columns(w[0]), by_columns(w[1].transpose(0, 2, 1)), by_columns(w[2])], axis=1),
        "bias": stack("bias_k", 1),
        "conv": conv.reshape(P, G, SHIFTS, P),
        "c_weight": by_phase(a["L1_cond_c_weight"].T),
    }
    nc = bacc.Bacc("TRN2", target_bir_lowering=False, num_devices=1)
    arrays, args = {}, []
    for name in _INS:
        v = np.ascontiguousarray(laid[name])
        arrays[f"in_{name}_dram"] = v
        args.append(nc.dram_tensor(f"in_{name}_dram", v.shape, mybir.dt.from_np(v.dtype), kind="ExternalInput").ap())
    args.append(nc.dram_tensor("out_dram", (B, P, PH, T), F32, kind="ExternalOutput").ap())
    cond_resid_kernel(nc, *args)
    got = run_bass_kernel_spmd(nc, [arrays], core_ids=[0]).results[0]["out_dram"]
    return np.ascontiguousarray(got.transpose(0, 1, 3, 2)).reshape(B, P, L)
```

```python
from contextlib import ExitStack

import concourse.bass as bass
from concourse import mybir

F32 = mybir.dt.float32
F32R = mybir.dt.float32r
ALU = mybir.AluOpType
ACT = mybir.ActivationFunctionType
AX_X = mybir.AxisListType.X

P = 128
B = 32
L = 2048
K = 8
PH = 4
G = 4
CG = P // G
T = L // PH
TAPS = 9
SHIFTS = 3
NL = 3
OG = 16
NOG = P // OG
NETS = (range(0, 1), range(1, NL))
EARLY_MIXES = 11
MIXES_AHEAD = 3
DMA = 16
PAIR = 2
UNITS = B // PAIR * PH

X_LOAD, X_SPLIT, LAYER0, X1_SPLIT, CONV, X2_SPLIT, OUTPUT, STORE = 8, 7, 6, 1, 0, -5, -6, -7
FIRST, LAST = -X_LOAD, UNITS - 1 - STORE
BODY = 8
LOOP_FROM, LOOP_TO = 2 * BODY, UNITS - BODY - 1

C_C0, C_D, C_E = 0, 4, 12
COLS = 16

N_COND, N_W0, N_B0, N_B1 = 0, B, B + NL * P, B + NL * P + NL
N_W1 = N_B1 + NL
N_W2 = N_W1 + NL * P
NET_COLS = N_W2 + NL * K


class Step:

    def __init__(self, i, r):
        self.i, self.r = i, r
        self.known = isinstance(i, int)
        self.u = BODY * i + r if self.known else None

    def has(self, lead):
        return not self.known or 0 <= self.u + lead < UNITS

    def is_first(self, lead, unit=0):
        return self.known and self.u + lead == unit

    def quarter(self, lead):
        return (self.r + lead) % PH

    def side(self, lead):
        return (self.r + lead) % 2

    def pair_side(self, lead):
        return (self.r + lead) // PH % 2

    def count(self, per, lead, extra=0):
        return self.i * (BODY * per) + (per * (self.r + lead) + extra)

    def uses(self, per, lead, extra=0):
        return self.i * (BODY // 2 * per) + (per * ((self.r + lead) // 2) + extra)

    def pairs(self, per, lead, extra=0):
        return self.i * (BODY // PH * per) + (per * ((self.r + lead) // PH) + extra)


def wait(eng, semaphore, value):
    if not isinstance(value, int) or value > 0:
        eng.wait_ge(semaphore, value)


def units_of(s, lead):
    unit = s.u + lead - (UNITS - 2 * PH) if s.known else -1
    if 0 <= unit < PH:
        late = [s.u + unit, s.u + unit + 1] if unit < PH // 2 else []
        return [Step(u // BODY, u % BODY) for u in late]
    return [s] if s.has(lead) else []


def vector_takes_x2_hi(s):
    return s.known and UNITS - 2 * PH <= s.u + X2_SPLIT < UNITS - PH


def scalar_hurries(s):
    return s.known and s.u + X2_SPLIT in (UNITS - 3, UNITS - 2)


def scalar_takes_x_hi(s):
    return s.known and s.u < -LAYER0 // 2


def has_spare(s, lead):
    return s.known and s.u + lead >= UNITS - 2


def of_last_pair(s, lead):
    return s.known and s.u + lead >= UNITS - PH


def y_of_unit(s, lead, y_sb, x_sb, x1_chan):
    if not of_last_pair(s, lead):
        return y_sb[s.side(lead)]
    return (x_sb + x1_chan)[s.quarter(lead)]


def of_unit(s, lead, buffers, spares):
    return (spares if has_spare(s, lead) else buffers)[s.side(lead)]


def share(s, total, first, end):
    if not s.known or not first <= s.u < end:
        return range(0)
    return range(total * (s.u - first) // (end - first), total * (s.u + 1 - first) // (end - first))


def mixes_of(s):
    return [EARLY_MIXES + n for n in share(s, NL * NOG - EARLY_MIXES, -LAYER0, -LAYER0 // 2)]


def pairs_of(s):
    return share(s, B // PAIR, -LAYER0 // 2, 0)


def run_steps(eng, body, first=FIRST):
    for u in range(first, LOOP_FROM):
        body(Step(u // BODY, u % BODY))
    with eng.Fori(LOOP_FROM // BODY, (LOOP_TO + 1) // BODY) as i:
        for r in range(BODY):
            body(Step(i, r))
    for u in range(LOOP_TO + 1, LAST + 1):
        body(Step(u // BODY, u % BODY))


def cond_resid_kernel(nc, x, net, b2, consts, mix, bias, conv, c_weight, w3, out):
    with ExitStack() as ctx:
        def sb(name, shape, dt=F32):
            return ctx.enter_context(nc.sbuf_tensor(name, shape, dt))

        def sem(name):
            return ctx.enter_context(nc.semaphore(name))

        def two(name, shape, dt=F32):
            return [sb(f"{name}{j}", shape, dt) for j in range(2)]

        x_sb = two("x_sb", [P, PAIR, T])
        x_hi = two("x_hi", [P, PAIR, T], F32R)
        x_lo = two("x_lo", [P, PAIR, T], F32R)
        x1_chan = two("x1_chan", [P, PAIR, T])
        x1_poly = two("x1_poly", [P, G, PAIR, T])
        x1_hi = two("x1_hi", [P, PAIR, T + 2], F32R)
        x1_lo = two("x1_lo", [P, PAIR, T + 2], F32R)
        x2_poly = two("x2_poly", [P, PAIR, T])
        x2_chan = two("x2_chan", [P, PH, PAIR, T])
        x2_hi = two("x2_hi", [P, PAIR, T], F32R)
        x2_lo = two("x2_lo", [P, PAIR, T], F32R)
        y_sb = two("y_sb", [P, PAIR, T])
        a0_hi = two("a0_hi", [P, PAIR, P], F32R)
        a0_lo = two("a0_lo", [P, PAIR, P], F32R)
        m_hi = two("m_hi", [P, PAIR, P], F32R)
        m_lo = two("m_lo", [P, PAIR, P], F32R)
        cur = two("cur", [P, COLS])
        a0_all = sb("a0_all", [P, B, P])
        m_all = sb("m_all", [P, B, P])
        conv_hi = sb("conv_hi", [P, G, SHIFTS, P], F32R)
        conv_lo = sb("conv_lo", [P, G, SHIFTS, P], F32R)
        c0_all = sb("c0_all", [P, B + PAIR])
        d_all = sb("d_all", [P, B, G])
        e_all = sb("e_all", [P, B])
        consts_sb = sb("consts_sb", [P, P + OG + G])
        eye_sb, mask_sb, fside_sb = consts_sb[:, 0:P], consts_sb[:, P:P + OG], consts_sb[:, P + OG:]
        b2_sb = sb("b2_sb", [1, NL * K])
        bias_sb = sb("bias_sb", [K, NL, P])
        att3_sb = sb("att3_sb", [P, B])
        ones_sb = sb("ones_sb", [1, B])
        hid0 = sb("hid0", [P, NL, B])
        hid1 = sb("hid1", [P, NL, B])
        lmax = sb("lmax", [B, NL])
        lsub = sb("lsub", [B, NL, K])
        lexp = sb("lexp", [B, NL, K])
        lsum = sb("lsum", [B, NL])
        linv = sb("linv", [B, NL])
        att = sb("att", [B, NL, K, OG])
        att_hi = sb("att_hi", [P, NL, B], F32R)
        att_lo = sb("att_lo", [P, NL, B])
        att_t = sb("att_t", [K, NL, B])
        c2_att = sb("c2_att", [P, NOG, B])

        def part(buf, pattern, at, size):
            return buf[:].rearrange(pattern)[:, at:at + size]

        late = (x1_poly[1], "p g b t -> p (g b t)")
        conv_f = part(*late, 0, G * SHIFTS * P).rearrange("p (g s m) -> p g s m", g=G, s=SHIFTS)
        at = G * SHIFTS * P
        cw_sb = part(*late, at, G * P).rearrange("p (g m) -> p g m", g=G)
        at += G * P
        w3_sb = part(*late, at, NOG * P).rearrange("p (g m) -> p g m", g=NOG)
        at += NOG * P
        bias2_rows = part(*late, at, NOG * P)[0:K].rearrange("p (g m) -> p g m", g=NOG)

        def halves(hi, lo, at):
            return [b[:, at:at + B * OG].rearrange("p (b o) -> p b o", b=B) for b in (hi, lo)]

        flat = "p b t -> p (b t)"
        spare = [buf[1][:].rearrange(flat) for buf in (x1_hi, x1_lo)]
        after_a0 = [buf[0][:].rearrange(flat) for buf in (x1_hi, x1_lo)]
        spread = [halves(*spare, 0), halves(*spare, B * OG), halves(*after_a0, 0)]

        def by_og(buf):
            return part(buf, flat, 0, NOG * P).rearrange("p (g m) -> p g m", g=NOG)

        mix_f = [by_og(y_sb[0]), by_og(x2_poly[0]), by_og(x2_poly[1])]
        mix_parts = [(by_og(x1_hi[0]), by_og(x1_lo[0])), (by_og(x2_hi[0]), by_og(x2_lo[0])),
                     (by_og(x2_hi[1]), by_og(x2_lo[1]))]
        net_sb = part(y_sb[1], flat, 0, NET_COLS)
        cond_sb = net_sb[:, N_COND:N_COND + B]
        w0_sb = net_sb[:, N_W0:N_W0 + NL * P].rearrange("p (n m) -> p n m", n=NL)
        w1_sb = net_sb[:, N_W1:N_W1 + NL * P].rearrange("p (n m) -> p n m", n=NL)
        w2_sb = net_sb[:, N_W2:N_W2 + NL * K].rearrange("p (n k) -> p n k", n=NL)
        b0_sb, b1_sb = net_sb[:, N_B0:N_B0 + NL], net_sb[:, N_B1:N_B1 + NL]
        a23_all = [buf[:].rearrange("p q b t -> p (q b t)").rearrange("p (n m) -> p n m", n=B)
                   for buf in x2_chan]

        def banks(name):
            return ctx.enter_context(nc.psum_tensor(name, [P, PAIR, 512], F32))

        l0_ps = banks("l0_ps")
        cv_ps = banks("cv_ps")
        y_ps = banks("y_ps")
        mix_ps = banks("mix_ps")

        net_loaded = sem("net_loaded")
        net2_loaded = sem("net2_loaded")
        consts_loaded = sem("consts_loaded")
        mix_loaded = [sem(f"mix_loaded{n}") for n in range(NL)]
        bias_loaded = sem("bias_loaded")
        conv_loaded = sem("conv_loaded")
        x_loaded = [sem(f"x_loaded{j}") for j in range(2)]
        remap1 = [sem(f"remap1_{j}") for j in range(2)]
        remap2 = [sem(f"remap2_{j}") for j in range(2)]
        last_rows = [sem(f"last_rows{p}") for p in range(PH)]
        stored = [sem(f"stored{j}") for j in range(2)]
        ones_set = sem("ones_set")
        chain = sem("chain")
        pool_chain = sem("pool_chain")
        h_made = [sem(f"h{n}_made") for n in range(2)]
        gelus = [sem(f"gelus{n}") for n in range(2)]
        logits_made = sem("logits_made")
        att_made = sem("att_made")
        att_t_made = sem("att_t_made")
        c_made = sem("c_made")
        e_made = sem("e_made")
        logits_less_max = sem("logits_less_max")
        att_ready = sem("att_ready")
        att_split = sem("att_split")
        att3_ready = sem("att3_ready")
        att_t_ready = sem("att_t_ready")
        spread_hi = [sem(f"spread_hi{n}") for n in range(NL)]
        spread_lo = [sem(f"spread_lo{n}") for n in range(NL)]
        mix_split = [sem(f"mix_split{n}") for n in range(NL)]
        exp_done = sem("exp_done")
        mix_made = sem("mix_made")
        mix_out = sem("mix_out")
        bias_out = sem("bias_out")
        m_made = sem("m_made")
        m_out = sem("m_out")
        e_loaded = sem("e_loaded")
        c2_att_ready = sem("c2_att_ready")
        e_out = sem("e_out")
        zero_cols = sem("zero_cols")
        zero_consts = sem("zero_consts")
        conv_split = sem("conv_split")
        cur_set = sem("cur_set")
        a0_split = sem("a0_split")
        m_split = sem("m_split")
        x_hi_done = sem("x_hi_done")
        x_lo_done = sem("x_lo_done")
        l0_done = sem("l0_done")
        x1_out = sem("x1_out")
        x1_hi_done = sem("x1_hi_done")
        x1_lo_done = sem("x1_lo_done")
        conv_done = sem("conv_done")
        x2_out = sem("x2_out")
        x2_hi_done = sem("x2_hi_done")
        x2_hi_last = sem("x2_hi_last")
        x2_lo_done = sem("x2_lo_done")
        x2_lo_last = sem("x2_lo_last")
        y_done = sem("y_done")
        y_out = sem("y_out")
        ROWS_DMA = 4 * DMA

        prep_ps = [mix_ps[:, 0, :], mix_ps[:, 1, :], cv_ps[:, 0, :], cv_ps[:, 1, :]]
        RING = len(prep_ps)
        y_banks = [y_ps, mix_ps]

        h_ps = [[cv_ps[:, h, 0:B]] + [y_ps[:, h, B * n:B * (n + 1)] for n in range(NL - 1)] for h in range(2)]
        logits_ps = [mix_ps[0:B, 0, 0:K].rearrange("b (n k) -> b n k", k=K),
                     y_ps[0:B, 0, 128:128 + (NL - 1) * K].rearrange("b (n k) -> b n k", k=K)]
        d_ps = y_ps[:, 1, 96:96 + G * B].rearrange("p (g n) -> p g n", g=G)
        c2_ps = y_ps[:, 1, 256:256 + NOG * B].rearrange("p (g n) -> p g n", g=NOG)
        c0_ps, e_ps = y_ps[:, 0, 256:256 + B], y_ps[:, 0, 256 + B:256 + 2 * B]
        att_ps = [l0_ps[:, 0, 0:B], l0_ps[:, 1, 0:B], l0_ps[:, 1, B:2 * B]]

        block = ctx.enter_context(nc.Block())

        x2_hi_end = [buf[:, :, 0:T] for buf in x1_hi]
        x2_lo_end = [buf[:, :, 0:T] for buf in x1_lo]

        def rows_back(eng, s):
            p = s.quarter(X2_SPLIT)
            if s.known and s.u + X2_SPLIT >= UNITS - PH:
                eng.wait_ge(remap2[0], ROWS_DMA * (UNITS // 2))
                eng.wait_ge(remap2[1], ROWS_DMA * (UNITS // 2 - 1))
                eng.wait_ge(last_rows[p], DMA)
            elif p == 0:
                for h in range(2):
                    eng.wait_ge(remap2[h], s.uses(ROWS_DMA, X2_SPLIT, 2 * ROWS_DMA))

        def split_x2_hi(eng, s, op, *identity):
            rows_back(eng, s)
            to = of_unit(s, X2_SPLIT, x2_hi, x2_hi_end)
            if not has_spare(s, X2_SPLIT):
                wait(eng, y_done, s.count(2, X2_SPLIT, -2))
            op(to[:], x2_chan[s.pair_side(X2_SPLIT)][:, s.quarter(X2_SPLIT)], *identity).then_inc(
                x2_hi_last if scalar_hurries(s) else x2_hi_done, 1)

        @block.sync
        def _(sp):
            def load(s):
                wait(sp, x_lo_done, s.count(1, X_LOAD, -1))
                sp.dma_start(x_sb[s.side(X_LOAD)][:],
                             x[bass.ds(s.pairs(PAIR, X_LOAD), PAIR), :, s.quarter(X_LOAD), :].rearrange(
                                 "b c t -> c b t")).then_inc(x_loaded[s.side(X_LOAD)], DMA)

            def store(s):
                if of_last_pair(s, STORE):
                    for k in range(PAIR):
                        sp.wait_ge(y_out, s.count(2, STORE, k + 1))
                        sp.dma_start(out[s.pairs(PAIR, STORE, k), :, s.quarter(STORE), :],
                                     y_of_unit(s, STORE, y_sb, x_sb, x1_chan)[:, k, :]).then_inc(stored[s.side(STORE)], DMA)
                    return
                wait(sp, y_out, s.count(2, STORE, 2))
                sp.dma_start(out[bass.ds(s.pairs(PAIR, STORE), PAIR), :, s.quarter(STORE), :].rearrange(
                    "b c t -> c b t"), y_of_unit(s, STORE, y_sb, x_sb, x1_chan)[:]).then_inc(stored[s.side(STORE)], DMA)

            sp.dma_start(net_sb[:, :N_W1], net[:, :N_W1]).then_inc(net_loaded, DMA)
            sp.dma_start(net_sb[:, N_W1:], net[:, N_W1:]).then_inc(net2_loaded, DMA)
            sp.dma_start(b2_sb[:], b2).then_inc(net2_loaded, DMA)
            sp.dma_start(consts_sb[:], consts).then_inc(consts_loaded, DMA)
            sp.dma_start(mix_f[0], mix[:, 0]).then_inc(mix_loaded[0], DMA)
            sp.dma_start(cw_sb, c_weight).then_inc(bias_loaded, DMA)
            sp.dma_start(bias_sb[:], bias[:, :NL * P].rearrange("k (n m) -> k n m", n=NL)).then_inc(bias_loaded, DMA)
            load(Step(-1, 0))
            for n in range(1, NL):
                sp.dma_start(mix_f[n], mix[:, n]).then_inc(mix_loaded[n], DMA)
            sp.dma_start(bias2_rows, bias[:, NL * P:].rearrange("k (g m) -> k g m", g=NOG)).then_inc(e_loaded, DMA)
            sp.dma_start(w3_sb, w3).then_inc(e_loaded, DMA)
            sp.dma_start(conv_f, conv).then_inc(conv_loaded, DMA)

            def step(s):
                if s.has(X_LOAD):
                    load(s)
                if s.has(LAYER0):
                    q, j = s.quarter(LAYER0), s.side(LAYER0)
                    wait(sp, x1_out, s.count(2, LAYER0, 2))
                    for g in range(G):
                        sp.dma_start(x1_poly[s.pair_side(LAYER0)][CG * q:CG * (q + 1), g],
                                     x1_chan[j][CG * g:CG * (g + 1)]).then_inc(remap1[j], DMA)
                for t in units_of(s, STORE):
                    store(t)
                if s.has(CONV):
                    g, j = s.quarter(CONV), s.side(CONV)
                    wait(sp, x2_out, s.count(2, CONV, 2))
                    for p in range(PH):
                        sp.dma_start(x2_chan[s.pair_side(CONV)][CG * g:CG * (g + 1), p],
                                     x2_poly[j][CG * p:CG * (p + 1)]).then_inc(
                                         last_rows[p] if s.is_first(CONV, UNITS - 1) else remap2[j], DMA)

            run_steps(sp, step, FIRST + 1)
            for j in range(2):
                sp.wait_ge(stored[j], DMA * ((UNITS - PH) // 2 + PAIR * PH // 2))

        @block.tensor
        def _(pe):
            def hidden(layer, nets):
                pe.wait_ge(net2_loaded if layer else net_loaded, 2 * DMA if layer else DMA)
                for n in nets:
                    if layer:
                        pe.wait_ge(gelus[0], n + 1)
                    w, a = (w1_sb[:, n, :], hid0[:, n, :]) if layer else (w0_sb[:, n, :], cond_sb)
                    pe.matmul(h_ps[layer][n], w, a, start=True, stop=True).then_inc(h_made[layer], 1)

            def logits(part):
                nets = NETS[part]
                ps = logits_ps[part]
                pe.wait_ge(ones_set, 1)
                pe.matmul(ps.rearrange("b n k -> b (n k)"), ones_sb[:], b2_sb[:, K * nets.start:K * nets.stop],
                          start=True, stop=False, skip_group_check=True)
                for n in nets:
                    pe.wait_ge(gelus[1], n + 1)
                    mm = pe.matmul(ps[:, n - nets.start, :], hid1[:, n, :], w2_sb[:, n, :], start=False, stop=True,
                                   skip_group_check=True)
                mm.then_inc(logits_made, 1)

            def attention(part):
                pe.wait_ge(consts_loaded, DMA)
                pe.wait_ge(att_ready, part + 1)
                for n in NETS[part]:
                    mm = pe.matmul(att_ps[n], att[:, n].rearrange("b k o -> b (k o)"), eye_sb[0:B, 0:B], start=True,
                                   stop=True)
                mm.then_inc(att_made, 1)

            def bias_d(groups):
                pe.wait_ge(bias_loaded, 2 * DMA)
                for g in groups:
                    pe.matmul(d_ps[:, g, :], cw_sb[:, g, :], cond_sb, start=True, stop=True)

            def keep_clock(products):
                for _ in range(products):
                    pe.matmul(l0_ps[:, 0, 0:SHIFTS * P], conv_hi[:, 0, 0, :],
                              conv_hi[:, 0].rearrange("p s m -> p (s m)"), start=True, stop=True)

            def mixture(n):
                layer, o = n // NOG, n % NOG
                if o == 0:
                    pe.wait_ge(mix_split[layer], 2)
                    pe.wait_ge(spread_hi[layer], 1)
                wait(pe, mix_out, n + 1 - RING)
                (w_hi, w_lo), (a_hi, a_lo) = mix_parts[layer], spread[layer]
                for k, (w, a) in enumerate(((w_hi, a_hi), (w_lo, a_hi), (w_hi, a_lo))):
                    if o == 0 and k == 2:
                        pe.wait_ge(spread_lo[layer], 1)
                    mm = pe.matmul(prep_ps[n % RING], w[:, o, :], a.rearrange("p b o -> p (b o)"), start=(k == 0),
                                   stop=(k == 2))
                mm.then_inc(mix_made, 1)

            def pair_product(m):
                if m == 0:
                    pe.wait_ge(mix_out, NL * NOG)
                wait(pe, m_out, m + 1 - RING)
                for k in range(PAIR):
                    n = PAIR * m + k
                    mm = pe.matmul(prep_ps[m % RING][:, P * k:P * (k + 1)], a23_all[0][:, n, :], a23_all[1][:, n, :],
                                   start=True, stop=True)
                mm.then_inc(m_made, 1)

            hidden(0, NETS[0])
            hidden(0, NETS[1])
            hidden(1, NETS[0])
            logits(0)
            attention(0)
            bias_d(range(0, G // 2))
            hidden(1, NETS[1])
            mixture(0)
            logits(1)
            for n in range(1, MIXES_AHEAD):
                mixture(n)
            attention(1)
            for n in range(NL):
                mm = pe.matmul(l0_ps[0:K, 1, 128 + B * n:128 + B * (n + 1)], att[:, n, :, 0], eye_sb[0:B, 0:B],
                               start=True, stop=True)
            mm.then_inc(att_t_made, 1)
            for n in range(MIXES_AHEAD, NOG):
                mixture(n)
            bias_d(range(G // 2, G))
            pe.wait_ge(att_t_ready, 1)
            pe.matmul(c0_ps, bias_sb[:, 0, :], att_t[:, 0, :], start=True, stop=True)
            pe.wait_ge(e_loaded, 2 * DMA)
            for i, n in enumerate(range(NOG, EARLY_MIXES)):
                for g in range(NOG * i // (EARLY_MIXES - NOG), NOG * (i + 1) // (EARLY_MIXES - NOG)):
                    mm = pe.matmul(c2_ps[:, g, :], bias2_rows[:, g, :], att_t[:, 1, :], start=True, stop=True)
                if n == EARLY_MIXES - 1:
                    mm.then_inc(c_made, 1)
                mixture(n)

            def bias_e(groups):
                if groups.start == 0:
                    pe.wait_ge(c2_att_ready, 1)
                    pe.wait_ge(bias_out, 2)
                    for n in range(1, NL):
                        pe.matmul(e_ps, bias_sb[:, n, :], att_t[:, n, :], start=(n == 1), stop=False)
                for g in groups:
                    mm = pe.matmul(e_ps, w3_sb[:, g, :], c2_att[:, g, :], start=False, stop=(g == NOG - 1))
                if groups.stop == NOG:
                    mm.then_inc(e_made, 1)

            def layer0(s):
                pe.wait_ge(x_lo_done, s.count(1, LAYER0, 1))
                if s.quarter(LAYER0) == 0:
                    pe.wait_ge(a0_split, s.pairs(2, LAYER0, 2))
                if s.is_first(LAYER0):
                    pe.wait_ge(att_split, 4)
                    pe.wait_ge(att3_ready, 1)
                    pe.wait_ge(att_t_ready, 1)
                j, m = s.side(LAYER0), s.pair_side(LAYER0)
                for k in range(PAIR):
                    wait(pe, x1_out, s.count(2, LAYER0, k - 1))
                    for n, (w, a) in enumerate(((a0_hi, x_hi), (a0_lo, x_hi), (a0_hi, x_lo))):
                        mm = pe.matmul(l0_ps[:, k, 0:T], w[m][:, k, :], a[j][:, k, :], start=(n == 0), stop=(n == 2))
                    mm.then_inc(l0_done, 1)

            def convolve(s):
                pe.wait_ge(x1_lo_done, s.count(1, CONV, 1))
                if s.is_first(CONV):
                    pe.wait_ge(conv_split, 2)
                    pe.wait_ge(zero_cols, 4)
                    pe.wait_ge(m_out, B // PAIR)
                j, g = s.side(CONV), s.quarter(CONV)
                for k in range(PAIR):
                    wait(pe, x2_out, s.count(2, CONV, k - 1))
                    n = 0
                    for sh in range(SHIFTS):
                        for w, a in ((conv_hi, x1_hi), (conv_lo, x1_hi), (conv_hi, x1_lo)):
                            mm = pe.matmul(cv_ps[:, k, 0:T], w[:, g, sh, :], a[j][:, k, sh:sh + T],
                                           start=(n == 0), stop=(n == 3 * SHIFTS - 1))
                            n += 1
                    mm.then_inc(conv_done, 1)

            def output(s):
                ps = y_banks[s.side(OUTPUT)]
                hi, lo = of_unit(s, OUTPUT, x2_hi, x2_hi_end), of_unit(s, OUTPUT, x2_lo, x2_lo_end)
                if not of_last_pair(s, OUTPUT):
                    pe.wait_ge(x2_lo_done, s.count(1, OUTPUT, 1))
                if s.quarter(OUTPUT) == 0:
                    pe.wait_ge(m_split, s.pairs(2, OUTPUT, 2))
                m = s.pair_side(OUTPUT)
                for k in range(PAIR):
                    if of_last_pair(s, OUTPUT):
                        pe.wait_ge(x2_lo_last, PAIR * (s.u + OUTPUT - (UNITS - PH)) + k + 1)
                    wait(pe, y_out, s.count(2, OUTPUT, k - 3))
                    for n, (w, a) in enumerate(((m_hi, hi), (m_lo, hi), (m_hi, lo))):
                        mm = pe.matmul(ps[:, k, 0:T], w[m][:, k, :], a[:, k, :], start=(n == 0), stop=(n == 2))
                    mm.then_inc(y_done, 1)

            def step(s):
                if s.has(LAYER0):
                    layer0(s)
                if s.has(CONV):
                    convolve(s)
                for t in units_of(s, OUTPUT):
                    if t.is_first(OUTPUT, UNITS - PH):
                        keep_clock(10)
                    output(t)
                mixes = mixes_of(s)
                for i, n in enumerate(mixes):
                    mixture(n)
                    if s.is_first(LAYER0):
                        bias_e(range(NOG * i // len(mixes), NOG * (i + 1) // len(mixes)))
                for m in pairs_of(s):
                    pair_product(m)

            run_steps(pe, step)

        @block.scalar
        def _(act):
            for part, nets in enumerate(NETS):
                for layer, (bias, to) in enumerate(((b0_sb, hid0), (b1_sb, hid1))):
                    act.wait_ge(h_made[layer], nets.stop)
                    for n in nets:
                        nc.scalar.activation(to[:, n, :], h_ps[layer][n], ACT.Gelu,
                                             bias=bias[:, n:n + 1]).then_inc(gelus[layer], 1)
                act.wait_ge(logits_less_max, part + 1)
                nc.scalar.activation(lexp[:, nets.start:nets.stop], lsub[:, nets.start:nets.stop],
                                     ACT.Exp).then_inc(exp_done, 1)

            def split_x_hi(s):
                j = s.side(X_SPLIT)
                act.wait_ge(x_loaded[j], s.uses(DMA, X_SPLIT, DMA))
                wait(act, l0_done, s.count(2, X_SPLIT, -2))
                nc.scalar.activation(x_hi[j][:], x_sb[j][:], ACT.Identity).then_inc(x_hi_done, 1)

            for n in range(1, NL):
                if n == NL - 1:
                    split_x_hi(Step(-1, BODY - X_SPLIT))
                act.wait_ge(mix_loaded[n], DMA)
                nc.scalar.activation(mix_parts[n][0], mix_f[n], ACT.Identity).then_inc(mix_split[n], 1)

            def evacuate_y(s):
                c = cur[s.pair_side(0)]
                y = y_of_unit(s, OUTPUT, y_sb, x_sb, x1_chan)
                if not of_last_pair(s, OUTPUT):
                    wait(act, stored[s.side(OUTPUT)], s.uses(DMA, OUTPUT))
                for k in range(PAIR):
                    act.wait_ge(y_done, s.count(2, OUTPUT, k + 1))
                    col = C_E + PAIR * (((s.r % PH) + OUTPUT) // PH + 2) + k
                    nc.scalar.activation(y[:, k, :], y_banks[s.side(OUTPUT)][:, k, 0:T], ACT.Identity,
                                         bias=c[:, col:col + 1]).then_inc(y_out, 1)

            def step(s):
                c = cur[s.pair_side(0)]
                if scalar_takes_x_hi(s) and s.has(X_SPLIT) and not s.is_first(X_SPLIT):
                    split_x_hi(s)
                if s.known and s.u < -LAYER0:
                    return
                if s.r % PH == 0 or s.is_first(LAYER0):
                    act.wait_ge(cur_set, s.pairs(3, 0, 3 * 3))
                if s.has(LAYER0):
                    j = s.side(LAYER0)
                    wait(act, remap1[j], s.uses(ROWS_DMA, LAYER0))
                    if s.quarter(LAYER0) == 0:
                        wait(act, x1_lo_done, s.count(1, LAYER0, -PH))
                    if s.is_first(LAYER0, PH):
                        act.wait_ge(conv_split, 2)
                        act.wait_ge(mix_made, NL * NOG)
                    for k in range(PAIR):
                        act.wait_ge(l0_done, s.count(2, LAYER0, k + 1))
                        col = C_C0 + PAIR * (((s.r % PH) + LAYER0) // PH - 1) + k
                        nc.scalar.activation(x1_chan[j][:, k, :], l0_ps[:, k, 0:T], ACT.Identity,
                                             bias=c[:, col:col + 1]).then_inc(x1_out, 1)
                if s.is_first(X2_SPLIT, UNITS - PH):
                    for u in (s.u + 1, s.u + 2):
                        split_x2_hi(act, Step(u // BODY, u % BODY), nc.scalar.activation, ACT.Identity)
                elif s.has(X2_SPLIT) and not vector_takes_x2_hi(s) and not of_last_pair(s, X2_SPLIT):
                    split_x2_hi(act, s, nc.scalar.activation, ACT.Identity)
                if s.has(CONV):
                    j = s.side(CONV)
                    wait(act, remap2[j], s.uses(ROWS_DMA, CONV))
                    if s.quarter(CONV) == 0:
                        wait(act, x2_lo_done, s.count(1, CONV, -PH))
                    if s.is_first(CONV):
                        act.wait_ge(m_made, B // PAIR)
                    for k in range(PAIR):
                        act.wait_ge(conv_done, s.count(2, CONV, k + 1))
                        col = C_D + G * k + s.quarter(CONV)
                        nc.scalar.activation(x2_poly[j][:, k, :], cv_ps[:, k, 0:T], ACT.Identity,
                                             bias=c[:, col:col + 1]).then_inc(x2_out, 1)
                for t in units_of(s, OUTPUT):
                    if t.u != s.u:
                        act.wait_ge(cur_set, t.pairs(3, 0, 3 * 3))
                    evacuate_y(t)
                for m in pairs_of(s):
                    act.wait_ge(m_made, m + 1)
                    nc.scalar.activation(m_all[:, PAIR * m:PAIR * (m + 1), :].rearrange("p n m -> p (n m)"),
                                         prep_ps[m % RING][:, 0:PAIR * P], ACT.Identity).then_inc(m_out, 1)

            run_steps(act, step)

        @block.gpsimd
        def _(pool):
            nc.gpsimd.memset(ones_sb[:], 1.0).then_inc(ones_set, 1)
            for j in range(2):
                nc.gpsimd.memset(cur[j][:], 0.0).then_inc(zero_consts, 1)
            nc.gpsimd.memset(c0_all[:, B:], 0.0).then_inc(zero_consts, 1)

            def spread_part(layer, half):
                src = (att_hi[:].bitcast(F32), att_lo[:])[half][:, layer, :]
                nc.gpsimd.tensor_tensor(spread[layer][half], src.unsqueeze(2).to_broadcast([P, B, OG]),
                                        mask_sb.unsqueeze(1).to_broadcast([P, B, OG]),
                                        ALU.mult).then_inc((spread_hi, spread_lo)[half][layer], 1)

            def set_cur(s):
                to = cur[s.pair_side(0)]
                base = s.pairs(PAIR, 0)
                for table, col, ahead, width, per in ((c0_all, C_C0, PAIR, 2 * PAIR, 1), (d_all, C_D, 0, PAIR, G),
                                                      (e_all, C_E, -2 * PAIR, 2 * PAIR, 1)):
                    lo, hi = 0, width
                    if s.known:
                        lo, hi = max(0, -(base + ahead)), min(width, B - (base + ahead))
                    if lo >= hi:
                        nc.gpsimd.memset(to[:, col:col + 1], 0.0).then_inc(cur_set, 1)
                        continue
                    src = table[:, bass.ds(base + (ahead + lo), hi - lo)]
                    dst = to[:, col + per * lo:col + per * hi]
                    if per > 1:
                        dst = dst.rearrange("p (n g) -> p n g", g=per)
                    nc.gpsimd.tensor_copy(dst, src).then_inc(cur_set, 1)

            def split_mix_lo(n):
                pool.wait_ge(mix_loaded[n], DMA)
                pool.wait_ge(mix_split[n], 1)
                nc.gpsimd.tensor_tensor(mix_parts[n][1], mix_f[n], mix_parts[n][0].bitcast(F32),
                                        ALU.subtract).then_inc(mix_split[n], 1)

            split_mix_lo(0)
            pool.wait_ge(consts_loaded, DMA)
            pool.wait_ge(att_split, 2)
            spread_part(0, 1)
            split_mix_lo(1)
            pool.wait_ge(att_split, 4)
            spread_part(1, 0)
            spread_part(1, 1)
            split_mix_lo(2)
            pool.wait_ge(zero_consts, 3)
            pool.wait_ge(bias_out, 2)
            set_cur(Step(-1, 0))
            pool.wait_ge(mix_made, NOG)
            spread_part(2, 0)
            spread_part(2, 1)

            def step(s):
                if s.is_first(X_SPLIT):
                    pool.wait_ge(conv_loaded, DMA)
                    nc.gpsimd.tensor_tensor(conv_f[:, :, 1, :], conv_f[:, :, 1, :],
                                            eye_sb.unsqueeze(1).to_broadcast([P, G, P]), ALU.add).then_inc(pool_chain, 1)
                    pool.wait_ge(pool_chain, 1)
                    nc.gpsimd.tensor_copy(conv_hi[:], conv_f).then_inc(conv_split, 1)
                    pool.wait_ge(conv_split, 1)
                    nc.gpsimd.tensor_tensor(conv_lo[:], conv_f, conv_hi[:].bitcast(F32),
                                            ALU.subtract).then_inc(conv_split, 1)
                    pool.wait_ge(mix_made, NL * NOG)
                    for j in range(2):
                        for buf in (x1_hi[j], x1_lo[j]):
                            nc.gpsimd.memset(buf[:, :, 0:T + 2:T + 1].bitcast(F32), 0.0).then_inc(zero_cols, 1)
                if s.r % PH:
                    return
                if s.is_first(0):
                    pool.wait_ge(e_out, 1)
                ahead = Step(s.i, s.r + PH) if not s.known else Step((s.u + PH) // BODY, (s.u + PH) % BODY)
                if s.known and s.u + PH > LAST:
                    return
                if not s.known:
                    pool.wait_ge(x1_out, s.count(2, LAYER0, 0))
                    pool.wait_ge(x2_out, s.count(2, CONV, 0))
                    pool.wait_ge(y_out, s.count(2, OUTPUT, 0))
                else:
                    for done, lead in ((x1_out, LAYER0), (x2_out, CONV), (y_out, OUTPUT)):
                        wait(pool, done, 2 * min(s.u + lead, UNITS))
                set_cur(ahead)

            run_steps(pool, step, -BODY)

        @block.vector
        def _(dve):
            steps = [0]

            def after(ins):
                steps[0] += 1
                ins.then_inc(chain, 1)
                dve.wait_ge(chain, steps[0])

            def mix_evacuate(n):
                layer, o = n // NOG, n % NOG
                to = a0_all if layer == 0 else a23_all[layer - 1]
                dve.wait_ge(mix_made, n + 1)
                nc.vector.tensor_tensor(to[:, :, OG * o:OG * (o + 1)],
                                        prep_ps[n % RING].rearrange("p (b o) -> p b o", b=B),
                                        eye_sb[:, OG * o:OG * (o + 1)].unsqueeze(1).to_broadcast([P, B, OG]),
                                        ALU.add).then_inc(mix_out, 1)

            def split_x(s):
                j = s.side(X_SPLIT)
                dve.wait_ge(x_loaded[j], s.uses(DMA, X_SPLIT, DMA))
                wait(dve, l0_done, s.count(2, X_SPLIT, -2))
                if not scalar_takes_x_hi(s):
                    nc.vector.tensor_copy(x_hi[j][:], x_sb[j][:]).then_inc(x_hi_done, 1)
                dve.wait_ge(x_hi_done, s.count(1, X_SPLIT, 1))
                nc.vector.tensor_tensor(x_lo[j][:], x_sb[j][:], x_hi[j][:].bitcast(F32),
                                        ALU.subtract).then_inc(x_lo_done, 1)

            def split_weights(s, lead, every, hi, lo, done, reader):
                m = s.pair_side(lead)
                src = every[:, bass.ds(s.pairs(PAIR, lead), PAIR), :]
                wait(dve, reader, s.count(2, lead, -2 * PH))
                nc.vector.tensor_scalar(hi[m][:], src, 1.0, None, ALU.mult).then_inc(done, 1)
                dve.wait_ge(done, s.pairs(2, lead, 1))
                nc.vector.tensor_tensor(lo[m][:], src, hi[m][:].bitcast(F32), ALU.subtract).then_inc(done, 1)

            def split_x2_lo(s):
                m, p = s.pair_side(X2_SPLIT), s.quarter(X2_SPLIT)
                if p == 0:
                    if s.is_first(X2_SPLIT):
                        dve.wait_ge(m_out, B // PAIR)
                    split_weights(s, X2_SPLIT, m_all, m_hi, m_lo, m_split, y_done)
                rows_back(dve, s)
                hi, lo = of_unit(s, X2_SPLIT, x2_hi, x2_hi_end), of_unit(s, X2_SPLIT, x2_lo, x2_lo_end)
                if of_last_pair(s, X2_SPLIT):
                    if scalar_hurries(s):
                        dve.wait_ge(x2_hi_last, s.u + X2_SPLIT - (UNITS - PH))
                    if not has_spare(s, X2_SPLIT):
                        dve.wait_ge(y_done, s.count(2, X2_SPLIT, -2))
                    for k in range(PAIR):
                        if not scalar_hurries(s):
                            after(nc.vector.tensor_copy(hi[:, k, :], x2_chan[m][:, p, k]))
                        nc.vector.tensor_tensor(lo[:, k, :], x2_chan[m][:, p, k], hi[:, k, :].bitcast(F32),
                                                ALU.subtract).then_inc(x2_lo_last, 1)
                    return
                if vector_takes_x2_hi(s):
                    split_x2_hi(dve, s, nc.vector.tensor_copy)
                dve.wait_ge(x2_hi_done, s.count(1, X2_SPLIT, 1))
                wait(dve, y_done, s.count(2, X2_SPLIT, -2))
                nc.vector.tensor_tensor(lo[:], x2_chan[m][:, p], hi[:].bitcast(F32),
                                        ALU.subtract).then_inc(x2_lo_done, 1)

            def step(s):
                if s.has(X1_SPLIT):
                    j, m, g = s.side(X1_SPLIT), s.pair_side(X1_SPLIT), s.quarter(X1_SPLIT)
                    if g == 0:
                        for h in range(2):
                            dve.wait_ge(remap1[h], s.uses(ROWS_DMA, X1_SPLIT, 2 * ROWS_DMA))
                    wait(dve, conv_done, s.count(2, X1_SPLIT, -2))
                    nc.vector.tensor_copy(x1_hi[j][:, :, 1:T + 1], x1_poly[m][:, g]).then_inc(x1_hi_done, 1)
                    dve.wait_ge(x1_hi_done, s.count(1, X1_SPLIT, 1))
                    nc.vector.tensor_tensor(x1_lo[j][:, :, 1:T + 1], x1_poly[m][:, g],
                                            x1_hi[j][:, :, 1:T + 1].bitcast(F32), ALU.subtract).then_inc(x1_lo_done, 1)
                if s.has(X_SPLIT) and not s.is_first(X_SPLIT):
                    split_x(s)
                    if s.quarter(X_SPLIT) == 0:
                        split_weights(s, X_SPLIT, a0_all, a0_hi, a0_lo, a0_split, l0_done)
                for t in units_of(s, X2_SPLIT):
                    split_x2_lo(t)
                for n in mixes_of(s):
                    mix_evacuate(n)
                if s.is_first(LAYER0, 1):
                    dve.wait_ge(e_made, 1)
                    nc.vector.tensor_copy(e_all[:], e_ps).then_inc(e_out, 1)

            def less_maximum(part):
                nets = slice(NETS[part].start, NETS[part].stop)
                dve.wait_ge(logits_made, part + 1)
                after(nc.vector.tensor_reduce(lmax[:, nets], logits_ps[part], AX_X, ALU.max))
                nc.vector.tensor_tensor(lsub[:, nets], logits_ps[part],
                                        lmax[:, nets].unsqueeze(2).to_broadcast([B, len(NETS[part]), K]),
                                        ALU.subtract).then_inc(logits_less_max, 1)

            def normalise(part):
                nets = slice(NETS[part].start, NETS[part].stop)
                shape = [B, len(NETS[part]), K, OG]
                dve.wait_ge(exp_done, part + 1)
                after(nc.vector.tensor_reduce(lsum[:, nets], lexp[:, nets], AX_X, ALU.add))
                after(nc.vector.reciprocal(linv[:, nets], lsum[:, nets]))
                nc.vector.tensor_tensor(att[:, nets], lexp[:, nets].unsqueeze(3).to_broadcast(shape),
                                        linv[:, nets].unsqueeze(2).unsqueeze(3).to_broadcast(shape),
                                        ALU.mult).then_inc(att_ready, 1)

            def split_att(part, src, nets):
                dve.wait_ge(att_made, part + 1)
                nc.vector.tensor_copy(att_hi[:, nets], src).then_inc(att_split, 1)
                dve.wait_ge(att_split, 2 * part + 1)
                nc.vector.tensor_tensor(att_lo[:, nets], src, att_hi[:, nets].bitcast(F32),
                                        ALU.subtract).then_inc(att_split, 1)

            less_maximum(0)
            dve.wait_ge(mix_loaded[0], DMA)
            nc.vector.tensor_copy(mix_parts[0][0], mix_f[0]).then_inc(mix_split[0], 1)
            normalise(0)
            split_att(0, att_ps[0], 0)
            dve.wait_ge(consts_loaded, DMA)
            nc.vector.tensor_tensor(spread[0][0], att_hi[:, 0, :].bitcast(F32).unsqueeze(2).to_broadcast([P, B, OG]),
                                    mask_sb.unsqueeze(1).to_broadcast([P, B, OG]), ALU.mult).then_inc(spread_hi[0], 1)
            mix_evacuate(0)
            less_maximum(1)
            normalise(1)
            for n in range(1, MIXES_AHEAD):
                mix_evacuate(n)
            dve.wait_ge(att_t_made, 1)
            split_att(1, l0_ps[:, 1, 0:2 * B].rearrange("p (n b) -> p n b", b=B), slice(1, NL))
            nc.vector.tensor_copy(att3_sb[:], att_ps[2]).then_inc(att3_ready, 1)
            nc.vector.tensor_copy(att_t[:], l0_ps[0:K, 1, 128:128 + NL * B].rearrange("k (n b) -> k n b",
                                                                                      n=NL)).then_inc(att_t_ready, 1)
            for n in range(MIXES_AHEAD, NOG):
                mix_evacuate(n)
                if n == NOG // 2:
                    split_x(Step(-1, BODY - X_SPLIT))
            dve.wait_ge(mix_out, NOG)
            split_weights(Step(-1, BODY - X_SPLIT), X_SPLIT, a0_all, a0_hi, a0_lo, a0_split, l0_done)
            dve.wait_ge(c_made, 1)
            nc.vector.tensor_copy(c0_all[:, 0:B], c0_ps).then_inc(bias_out, 1)
            nc.vector.tensor_tensor(d_all[:].rearrange("p n g -> p g n"), d_ps,
                                    fside_sb.unsqueeze(2).to_broadcast([P, G, B]), ALU.add).then_inc(bias_out, 1)
            dve.wait_ge(att3_ready, 1)
            nc.vector.tensor_tensor(c2_att[:], c2_ps, att3_sb[:].unsqueeze(1).to_broadcast([P, NOG, B]),
                                    ALU.mult).then_inc(c2_att_ready, 1)
            for n in range(NOG, EARLY_MIXES):
                mix_evacuate(n)
            run_steps(dve, step, -X_SPLIT)


_INS = ["x", "net", "b2", "consts", "mix", "bias", "conv", "c_weight", "w3"]


def kernel(**inputs):
    import numpy as np
    import concourse.bacc as bacc
    from concourse.bass_utils import run_bass_kernel_spmd

    a = {n: np.asarray(v) for n, v in inputs.items()}
    layers = ("L0", "L2", "L3")

    def stack(name, axis):
        return np.stack([a[f"{n}_cond_{name}"] for n in layers], axis=axis)

    taps = a["L1_cond_weight"].reshape(G, CG, CG, TAPS)
    conv = np.zeros((PH, CG, G, SHIFTS, PH, CG), np.float32)
    for s in range(SHIFTS):
        for q in range(PH):
            for p in range(PH):
                k = PH * (s - 1) + q - p + TAPS // 2
                if 0 <= k < TAPS:
                    conv[q, :, :, s, p, :] = taps[:, :, :, k].transpose(2, 0, 1)

    def by_phase(m):
        m = m.reshape(m.shape[0], G, 1, CG)
        return np.broadcast_to(m, (m.shape[0], G, PH, CG)).reshape(m.shape[0], G, P)

    def by_columns(m):
        return m.reshape(K, NOG, OG, P).transpose(0, 2, 1, 3).reshape(K * OG, NOG, P)

    w = [a[f"{n}_cond_weight"][..., 0] for n in layers]
    laid = {
        "x": a["x"].reshape(B, P, T, PH).transpose(0, 1, 3, 2),
        "net": np.concatenate([a["cond_128"].T, stack("W0", 1).reshape(P, NL * P), stack("b0", 1), stack("b1", 1),
                               stack("W1", 1).reshape(P, NL * P), stack("W2", 1).reshape(P, NL * K)], axis=1),
        "b2": stack("b2", 0).reshape(1, NL * K),
        "consts": np.concatenate([np.eye(P, dtype=np.float32), np.tile(np.eye(OG, dtype=np.float32), (K, 1)),
                                  by_phase(a["fside_S_0"].reshape(1, P))[0].T], axis=1),
        "mix": np.stack([by_columns(w[0]), by_columns(w[1].transpose(0, 2, 1)), by_columns(w[2])], axis=1),
        "bias": np.concatenate([stack("bias_k", 1).reshape(K, NL * P), np.broadcast_to(
            a["L2_cond_bias_k"].reshape(K, NOG, 1, OG), (K, NOG, K, OG)).reshape(K, NOG * P)], axis=1),
        "w3": by_columns(w[2].transpose(0, 2, 1)),
        "conv": conv.reshape(P, G, SHIFTS, P),
        "c_weight": by_phase(a["L1_cond_c_weight"].T),
    }
    nc = bacc.Bacc("TRN2", target_bir_lowering=False, num_devices=1)
    arrays, args = {}, []
    for name in _INS:
        v = np.ascontiguousarray(laid[name])
        arrays[f"in_{name}_dram"] = v
        args.append(nc.dram_tensor(f"in_{name}_dram", v.shape, mybir.dt.from_np(v.dtype), kind="ExternalInput").ap())
    args.append(nc.dram_tensor("out_dram", (B, P, PH, T), F32, kind="ExternalOutput").ap())
    cond_resid_kernel(nc, *args)
    got = run_bass_kernel_spmd(nc, [arrays], core_ids=[0]).results[0]["out_dram"]
    return np.ascontiguousarray(got.transpose(0, 1, 3, 2)).reshape(B, P, L)
```
